# Optimizing a Trainium2 kernel written in Bass

```python
import numpy as np
import jax
import jax.numpy as jnp

def _softmax(x, axis=-1):
    return jax.nn.softmax(x, axis=axis)

def _gelu(x):
    return jax.nn.gelu(x, approximate=True)

def _silu(x):
    return jax.nn.silu(x)

def _sigmoid(x):
    return jax.nn.sigmoid(x)

def _layernorm(x, axis=-1, eps=1e-05):
    m = jnp.mean(x, axis=axis, keepdims=True)
    v = jnp.var(x, axis=axis, keepdims=True)
    return (x - m) / jnp.sqrt(v + eps)

def _scatter_add(tgt, idx, src, axis=0):
    return tgt.at[idx].add(src)

def _segment_sum(src, seg, n):
    return jax.ops.segment_sum(src, seg, n)
kernel_name = 'mk_audio_tower_d1_tok_aud1d512_r4_65c2b7'

def setup_inputs(seed: int=0):
    np.random.seed(seed)
    _w = jnp.asarray

    def _rec_inputs():
        import jax
        import jax.numpy as jnp
        _rk = jax.random.key(seed)
        x = 0.00021031 + 1.00007 * jax.random.normal(jax.random.fold_in(_rk, 1), (32, 80000), jnp.float32)
        return x
    x = _rec_inputs()

    def _L0_tok_setup():
        import jax, jax.numpy as jnp
        import numpy as np
        FRAME_LENGTH = 256
        B, T = (16, 524288)

        def _mdct_matrix(length):
            L2 = length
            Lh = L2 // 2
            n = jnp.arange(L2, dtype=jnp.float32) + 0.5
            k = jnp.pi / Lh * n[:Lh]
            n = n + Lh / 2
            z = jnp.sqrt(jnp.float32(2.0 / Lh * 2.0))
            return z * jnp.cos(n[:, None] * k[None, :])
        key = jax.random.key(seed)
        x = jax.random.normal(key, (B, T), dtype=jnp.float32)
        return {'x': x}
    _L0_tok_all = _L0_tok_setup()
    _L0_tok_in = {k: v for k, v in _L0_tok_all.items() if k in ()}
    del _L0_tok_all

    def _L0_attn_setup():
        import jax, jax.numpy as jnp
        import numpy as np
        B, C, F, H, LOCAL_K = (32, 128, 128, 4, 5)
        DK = F // H
        EPS = 1e-05

        def _heads(x, W, b):
            y = x @ W.T + b
            Bn, Cn, _ = y.shape
            return y.reshape(Bn, Cn, H, DK).transpose(0, 2, 1, 3)

        def _merge(y):
            Bn, Hn, Cn, Dn = y.shape
            return y.transpose(0, 2, 1, 3).reshape(Bn, Cn, Hn * Dn)

        def _local_attn(Q, K, V, k):
            scale = jnp.sqrt(jnp.asarray(DK, Q.dtype))
            scores = jnp.einsum('bhcd,bhed->bhce', Q, K) / scale
            kth = jax.lax.top_k(scores, k)[0][..., -1:]
            masked = jnp.where(scores >= kth, scores, -jnp.inf)
            attn = jax.nn.softmax(masked, axis=-1)
            attn = jnp.nan_to_num(attn, nan=0.0)
            return jnp.einsum('bhce,bhed->bhcd', attn, V)

        def _global_attn(Q, K, V):
            scale = jnp.sqrt(jnp.asarray(DK, Q.dtype))
            scores = jnp.einsum('bhcd,bhed->bhce', Q, K) / scale
            attn = jax.nn.softmax(scores, axis=-1)
            return jnp.einsum('bhce,bhcd->bhed', attn.transpose(0, 1, 3, 2), V) if False else jnp.einsum('bhce,bhed->bhcd', attn, V)
        key = jax.random.key(seed)
        ks = jax.random.split(key, 20)
        s = 1.0 / np.sqrt(F)

        def lin(k):
            kw, kb = jax.random.split(k)
            W = jax.random.uniform(kw, (F, F), jnp.float32, -s, s)
            b = jax.random.uniform(kb, (F,), jnp.float32, -s, s)
            return (W, b)
        Wq1, bq1 = lin(ks[0])
        Wk1, bk1 = lin(ks[1])
        Wv1, bv1 = lin(ks[2])
        Wo1, bo1 = lin(ks[3])
        Wq2, bq2 = lin(ks[4])
        Wk2, bk2 = lin(ks[5])
        Wv2, bv2 = lin(ks[6])
        Wo2, bo2 = lin(ks[7])
        gamma = jnp.ones((F,), jnp.float32)
        beta = jnp.zeros((F,), jnp.float32)
        x = jax.random.normal(ks[8], (B, C, F), jnp.float32)
        return dict(x=x, Wq1=Wq1, bq1=bq1, Wk1=Wk1, bk1=bk1, Wv1=Wv1, bv1=bv1, Wo1=Wo1, bo1=bo1, Wq2=Wq2, bq2=bq2, Wk2=Wk2, bk2=bk2, Wv2=Wv2, bv2=bv2, Wo2=Wo2, bo2=bo2, gamma=gamma, beta=beta)
    _L0_attn_all = _L0_attn_setup()
    _L0_attn_in = {k: v for k, v in _L0_attn_all.items() if k in ('Wq1', 'bq1', 'Wk1', 'bk1', 'Wv1', 'bv1', 'Wo1', 'bo1', 'Wq2', 'bq2', 'Wk2', 'bk2', 'Wv2', 'bv2', 'Wo2', 'bo2', 'gamma', 'beta')}
    del _L0_attn_all

    def _L0_ffn_setup():
        import jax, jax.numpy as jnp
        import numpy as np
        MICRO_BATCHES = 2
        TOP_K = 2
        D = 128
        E = 8
        B, S = (8, 2048)
        key = jax.random.key(seed)
        ks = jax.random.split(key, 12)
        s = 0.02
        return {'x': jax.random.normal(ks[0], (B, S, D), dtype=jnp.float32), 'ln_g': jnp.ones((D,), jnp.float32), 'ln_b': jnp.zeros((D,), jnp.float32), 'attn_w': jax.random.normal(ks[1], (D, D), jnp.float32) * s, 'attn_b': jnp.zeros((D,), jnp.float32), 'gate_w': jax.random.normal(ks[2], (E, D), jnp.float32) * s, 'fc1_w': jax.random.normal(ks[3], (E, 4 * D, D), jnp.float32) * s, 'fc1_b': jnp.zeros((E, 4 * D), jnp.float32), 'fc2_w': jax.random.normal(ks[4], (E, D, 4 * D), jnp.float32) * s, 'fc2_b': jnp.zeros((E, D), jnp.float32), 'next_w': jax.random.normal(ks[5], (D, D), jnp.float32) * s, 'next_b': jnp.zeros((D,), jnp.float32)}
    _L0_ffn_all = _L0_ffn_setup()
    _L0_ffn_in = {k: v for k, v in _L0_ffn_all.items() if k in ('ln_g', 'ln_b', 'attn_w', 'attn_b', 'gate_w', 'fc1_w', 'fc1_b', 'fc2_w', 'fc2_b', 'next_w', 'next_b')}
    del _L0_ffn_all
    return {'x': x, 'L0_attn_Wq1': _L0_attn_in['Wq1'], 'L0_attn_bq1': _L0_attn_in['bq1'], 'L0_attn_Wk1': _L0_attn_in['Wk1'], 'L0_attn_bk1': _L0_attn_in['bk1'], 'L0_attn_Wv1': _L0_attn_in['Wv1'], 'L0_attn_bv1': _L0_attn_in['bv1'], 'L0_attn_Wo1': _L0_attn_in['Wo1'], 'L0_attn_bo1': _L0_attn_in['bo1'], 'L0_attn_Wq2': _L0_attn_in['Wq2'], 'L0_attn_bq2': _L0_attn_in['bq2'], 'L0_attn_Wk2': _L0_attn_in['Wk2'], 'L0_attn_bk2': _L0_attn_in['bk2'], 'L0_attn_Wv2': _L0_attn_in['Wv2'], 'L0_attn_bv2': _L0_attn_in['bv2'], 'L0_attn_Wo2': _L0_attn_in['Wo2'], 'L0_attn_bo2': _L0_attn_in['bo2'], 'L0_attn_gamma': _L0_attn_in['gamma'], 'L0_attn_beta': _L0_attn_in['beta'], 'L0_ffn_ln_g': _L0_ffn_in['ln_g'], 'L0_ffn_ln_b': _L0_ffn_in['ln_b'], 'L0_ffn_attn_w': _L0_ffn_in['attn_w'], 'L0_ffn_attn_b': _L0_ffn_in['attn_b'], 'L0_ffn_gate_w': _L0_ffn_in['gate_w'], 'L0_ffn_fc1_w': _L0_ffn_in['fc1_w'], 'L0_ffn_fc1_b': _L0_ffn_in['fc1_b'], 'L0_ffn_fc2_w': _L0_ffn_in['fc2_w'], 'L0_ffn_fc2_b': _L0_ffn_in['fc2_b'], 'L0_ffn_next_w': _L0_ffn_in['next_w'], 'L0_ffn_next_b': _L0_ffn_in['next_b']}

def reference(x, L0_attn_Wq1, L0_attn_bq1, L0_attn_Wk1, L0_attn_bk1, L0_attn_Wv1, L0_attn_bv1, L0_attn_Wo1, L0_attn_bo1, L0_attn_Wq2, L0_attn_bq2, L0_attn_Wk2, L0_attn_bk2, L0_attn_Wv2, L0_attn_bv2, L0_attn_Wo2, L0_attn_bo2, L0_attn_gamma, L0_attn_beta, L0_ffn_ln_g, L0_ffn_ln_b, L0_ffn_attn_w, L0_ffn_attn_b, L0_ffn_gate_w, L0_ffn_fc1_w, L0_ffn_fc1_b, L0_ffn_fc2_w, L0_ffn_fc2_b, L0_ffn_next_w, L0_ffn_next_b):
    import jax
    import jax.numpy as jnp

    def _L0_tok_ref(x):
        import jax, jax.numpy as jnp
        import numpy as np
        FRAME_LENGTH = 256
        B, T = (16, 524288)

        def _mdct_matrix(length):
            L2 = length
            Lh = L2 // 2
            n = jnp.arange(L2, dtype=jnp.float32) + 0.5
            k = jnp.pi / Lh * n[:Lh]
            n = n + Lh / 2
            z = jnp.sqrt(jnp.float32(2.0 / Lh * 2.0))
            return z * jnp.cos(n[:, None] * k[None, :])
        L = FRAME_LENGTH
        hop = L // 2
        xp = jnp.pad(x, ((0, 0), (L // 2, hop + (L - 1) // 2)))
        n_frames = (xp.shape[-1] - L) // hop + 1
        idx = jnp.arange(n_frames)[:, None] * hop + jnp.arange(L)[None, :]
        frames = xp[:, idx]
        w = jnp.sin(jnp.pi * (jnp.arange(L, dtype=jnp.float32) + 0.5) / L)
        Wm = _mdct_matrix(L)
        return jnp.einsum('bnl,lk->bnk', frames * w, Wm)

    def _L0_attn_ref(x, Wq1, bq1, Wk1, bk1, Wv1, bv1, Wo1, bo1, Wq2, bq2, Wk2, bk2, Wv2, bv2, Wo2, bo2, gamma, beta):
        import jax, jax.numpy as jnp
        import numpy as np
        B, C, F, H, LOCAL_K = (32, 128, 128, 4, 5)
        DK = F // H
        EPS = 1e-05

        def _heads(x, W, b):
            y = x @ W.T + b
            Bn, Cn, _ = y.shape
            return y.reshape(Bn, Cn, H, DK).transpose(0, 2, 1, 3)

        def _merge(y):
            Bn, Hn, Cn, Dn = y.shape
            return y.transpose(0, 2, 1, 3).reshape(Bn, Cn, Hn * Dn)

        def _local_attn(Q, K, V, k):
            scale = jnp.sqrt(jnp.asarray(DK, Q.dtype))
            scores = jnp.einsum('bhcd,bhed->bhce', Q, K) / scale
            kth = jax.lax.top_k(scores, k)[0][..., -1:]
            masked = jnp.where(scores >= kth, scores, -jnp.inf)
            attn = jax.nn.softmax(masked, axis=-1)
            attn = jnp.nan_to_num(attn, nan=0.0)
            return jnp.einsum('bhce,bhed->bhcd', attn, V)

        def _global_attn(Q, K, V):
            scale = jnp.sqrt(jnp.asarray(DK, Q.dtype))
            scores = jnp.einsum('bhcd,bhed->bhce', Q, K) / scale
            attn = jax.nn.softmax(scores, axis=-1)
            return jnp.einsum('bhce,bhcd->bhed', attn.transpose(0, 1, 3, 2), V) if False else jnp.einsum('bhce,bhed->bhcd', attn, V)
        Q1 = _heads(x, Wq1, bq1)
        K1 = _heads(x, Wk1, bk1)
        V1 = _heads(x, Wv1, bv1)
        local = _merge(_local_attn(Q1, K1, V1, min(LOCAL_K, C))) @ Wo1.T + bo1
        Q2 = _heads(local, Wq2, bq2)
        K2 = _heads(local, Wk2, bk2)
        V2 = _heads(local, Wv2, bv2)
        glob = _merge(_global_attn(Q2, K2, V2)) @ Wo2.T + bo2
        h = x + glob
        mu = jnp.mean(h, axis=-1, keepdims=True)
        var = jnp.var(h, axis=-1, keepdims=True)
        return (h - mu) / jnp.sqrt(var + EPS) * gamma + beta

    def _L0_ffn_ref(x, ln_g, ln_b, attn_w, attn_b, gate_w, fc1_w, fc1_b, fc2_w, fc2_b, next_w, next_b):
        import jax, jax.numpy as jnp
        import numpy as np
        MICRO_BATCHES = 2
        TOP_K = 2
        D = 128
        E = 8
        B, S = (8, 2048)
        b, s, d = x.shape
        xf = x.reshape(b * s, d)
        mu = jnp.mean(xf, axis=-1, keepdims=True)
        var = jnp.var(xf, axis=-1, keepdims=True)
        normed = (xf - mu) / jnp.sqrt(var + 1e-05) * ln_g + ln_b
        x_attn = normed @ attn_w.T + attn_b + xf
        logits = x_attn @ gate_w.T
        _scores, _indices = jax.lax.top_k(logits, TOP_K)
        e = fc1_w.shape[0]
        t = b * s // (MICRO_BATCHES * e)
        tok = x_attn.reshape(MICRO_BATCHES, e, t, d)
        h = jnp.einsum('meti,ehi->meth', tok, fc1_w) + fc1_b[None, :, None, :]
        h = jax.nn.gelu(h, approximate=False)
        y = jnp.einsum('meth,edh->metd', h, fc2_w) + fc2_b[None, :, None, :]
        yf = y.reshape(b * s, d)
        out = jax.nn.gelu(yf @ next_w.T + next_b, approximate=False)
        return out.reshape(b, s, d)
    h = _L0_tok_ref(x)
    h = h + _L0_attn_ref(_layernorm(h, axis=-1), L0_attn_Wq1, L0_attn_bq1, L0_attn_Wk1, L0_attn_bk1, L0_attn_Wv1, L0_attn_bv1, L0_attn_Wo1, L0_attn_bo1, L0_attn_Wq2, L0_attn_bq2, L0_attn_Wk2, L0_attn_bk2, L0_attn_Wv2, L0_attn_bv2, L0_attn_Wo2, L0_attn_bo2, L0_attn_gamma, L0_attn_beta)
    h = h + _L0_ffn_ref(_layernorm(h, axis=-1), L0_ffn_ln_g, L0_ffn_ln_b, L0_ffn_attn_w, L0_ffn_attn_b, L0_ffn_gate_w, L0_ffn_fc1_w, L0_ffn_fc1_b, L0_ffn_fc2_w, L0_ffn_fc2_b, L0_ffn_next_w, L0_ffn_next_b)
    return h

_drawn_inputs = setup_inputs


def setup_inputs(seed=0):
    import zlib

    import numpy as np

    out = dict(_drawn_inputs(seed))
    spreads = {'L0_attn_gamma': (1.0, 0.2),
     'L0_attn_beta': (0.0, 0.1),
     'L0_ffn_ln_g': (1.0, 0.6),
     'L0_ffn_ln_b': (0.0, 0.8),
     'L0_ffn_attn_b': (0.0, 0.8),
     'L0_ffn_fc1_b': (0.0, 0.8),
     'L0_ffn_fc2_b': (0.0, 0.8),
     'L0_ffn_next_b': (0.0, 2.0)}
    factors = {'L0_attn_Wq1': 8.0,
     'L0_attn_bq1': 8.0,
     'L0_attn_Wk1': 8.0,
     'L0_attn_bk1': 200.0,
     'L0_attn_Wv1': 8.0,
     'L0_attn_bv1': 8.0,
     'L0_attn_Wo1': 8.0,
     'L0_attn_bo1': 7.876,
     'L0_attn_Wq2': 8.0,
     'L0_attn_bq2': 8.0,
     'L0_attn_Wk2': 8.0,
     'L0_attn_bk2': 200.0,
     'L0_attn_Wv2': 5.454,
     'L0_attn_bv2': 180.212,
     'L0_attn_Wo2': 3.541,
     'L0_ffn_attn_w': 8.0,
     'L0_ffn_fc1_w': 8.0,
     'L0_ffn_fc2_w': 8.0,
     'L0_ffn_next_w': 8.0,
     'L0_attn_bo2': 64.0}
    for name, (base, spread) in spreads.items():
        noise = np.random.default_rng([zlib.crc32(name.encode()), seed]).standard_normal(out[name].shape)
        drawn = base * np.exp(spread * noise) if base else spread * noise
        out[name] = jnp.asarray(drawn.astype(out[name].dtype))
    for name, factor in factors.items():
        out[name] = (out[name] * factor).astype(out[name].dtype)
    return out
```

```python
from contextlib import ExitStack

import numpy as np

import concourse.bass as bass
from concourse import mybir

F32 = mybir.dt.float32
F32R = mybir.dt.float32r
ALU = mybir.AluOpType
ACT = mybir.ActivationFunctionType
AX = mybir.AxisListType

P = 128
C = 626
D = 128
H = 4
DK = D // H
TOPK = 5
NT = -(-C // P)
CP = NT * P
HID = 512
KH = HID // P
EPS = 1e-5
SCALE = float(DK) ** -0.5
TILES = NT * H
HALF = ((0, 384), (384, C - 384))
HALF_TILES = ((0, 1, 2), (3, 4))
S0, S1 = 198, 512
N0 = S1 - S0
STEPS = (4, 5 + NT, 8 + NT)
LAG = 2


def rows(t):
    return min(P, C - t * P)


class Iteration:

    def __init__(self, index, first=None):
        self.index, self.looped = index, first is not None
        self.like = first if self.looped else index

    def at(self, f):
        if not self.looped:
            return f(self.index)
        start, step = f(self.like), f(self.like + 1) - f(self.like)
        return self.index * step + (start - step * self.like)


class Plan:

    X, Y = 0, 1

    UNITS = {
        X: {
            0: [("mdct", 1, 0), ("mdct", 1, 1)],
            1: [("q2", -1, 0), ("q2", -1, 1)],
            2: [("k2", -1, 0), ("k2", -1, 1)],
            3: [("spread2", -2, 1), ("pv2", -2, 1)],
            8: [("wo2", -2, 0), ("wo2", -2, 1)],
            9: [("down", -3, 0)],
            10: [("down", -3, 1)],
            11: [("v2", -1, 0), ("v2", -1, 1)],
            12: [("next", -3, 0), ("next", -3, 1)],
            13: [("turn", 1, 0), ("turn", 1, 1)],
            15: [("spread1", 0, 0), ("pv1", 0, 0)],
        },
        Y: {
            0: [("q1", 1, 0), ("q1", 1, 1)],
            1: [("k1", 1, 0), ("k1", 1, 1)],
            2: [("turn_n", -2, 0), ("turn_n", -2, 1)],
            3: [("spread1", 0, 1), ("pv1", 0, 1)],
            8: [("mix", -2, 0), ("mix", -2, 1)],
            9: [("v1", 1, 0), ("v1", 1, 1)],
            10: [("up", -2, 0), ("up", -2, 1)],
            11: [("up", -2, 2), ("up", -2, 3)],
            12: [("up", -2, 4), ("up", -2, 5)],
            13: [("up", -2, 6), ("up", -2, 7)],
            15: [("spread2", -1, 0), ("pv2", -1, 0)],
        },
    }
    SPREAD_SLOTS = NT
    JOBS = {
        X: {1: [("inverse2", -2, 1), ("stats_h", 1, 0)], 9: [("stats_hh", -2, 0)],
            14: [("inverse1", 0, 0)], 16: [("stats_h2", -2, 0)]},
        Y: {1: [("inverse1", 0, 1)], 14: [("inverse2", -1, 0), ("gelu_out", -3, 0), ("gelu_up", -2, 0)]},
    }

    def __init__(self, batches):
        self.batches = batches
        self.loop = (4, batches - 2)
        self.unit_total = {}

    def has(self, it, offset):
        return it.looped or 0 <= it.like + offset < self.batches

    def phase_exists(self, j, phase):
        return 0 <= j - phase < self.batches

    def phases_before(self, j, phase=0):
        n = sum(self.phase_exists(i, q) for i in range(j) for q in (0, 1))
        return n + (phase == 1 and self.phase_exists(j, 0))

    def tile(self, it, phase, slot, lag=0):
        k, back = slot - lag, 0
        if k < 0:
            k += TILES
            phase, back = (0, 0) if phase == 1 else (1, 1)
        if not it.looped and not self.phase_exists(it.like - back, phase):
            return None
        return phase, -back - phase, k, back

    def number(self, it, tile):
        phase, _, k, back = tile
        return it.at(lambda j: TILES * self.phases_before(j - back, phase) + k)

    def half_number(self, it, phase, back):
        return it.at(lambda j: self.phases_before(j - back, phase))

    def slot_units(self, it, phase, slot):
        return [u for u in self.UNITS[phase].get(slot, []) if self.has(it, u[1])]

    def results(self, it, phase, slot):
        here = [(slot, n, u) for n, u in enumerate(self.slot_units(it, phase, slot)) if u[0][:2] != "pv"]
        first = slot - self.SPREAD_SLOTS + 1
        late = [(first, n, u) for n, u in enumerate(self.slot_units(it, phase, first)) if u[0][:2] == "pv"]
        return here + late

    def units_before(self, j, phase, slot, n):
        if j not in self.unit_total:
            self.unit_total[j] = sum(self.units_in(i, 2, 0) for i in range(-1, j))
        return self.unit_total[j] + self.units_in(j, phase, slot) + n

    def units_in(self, j, phase, slot):
        return sum(
            0 <= j + u[1] < self.batches
            for q in (0, 1) for s, us in self.UNITS[q].items() if (q, s) < (phase, slot) for u in us
        )

    def bank(self, it, phase, slot, n):
        u = self.units_before(it.like, phase, slot, n)
        return u % 2, it.at(lambda j: self.units_before(j, phase, slot, n) // 2), u < 2

    def place(self, name, part):
        for phase, slots in self.UNITS.items():
            for slot, units in slots.items():
                for n, u in enumerate(units):
                    if (u[0], u[2]) == (name, part):
                        return phase, slot, n, u[1]
        raise KeyError(name)

    def unit_count(self, it, offset, name, part):
        phase, slot, n, own = self.place(name, part)
        back = own - offset

        def number(j):
            present = self.UNITS[phase][slot][:n]
            before = sum(0 <= j + u[1] < self.batches for u in present)
            return self.units_before(j, phase, slot, before)

        u = number(it.like - back)
        return u % 2, it.at(lambda j: number(j - back) // 2 + 1)


def build(nc, xT, mats, cols, rows_in, experts, out):
    B = xT.shape[0]
    plan = Plan(B)
    X, Y = Plan.X, Plan.Y
    NM, NCOL, NROW = mats.shape[1], cols.shape[1], rows_in.shape[0]
    spill = nc.dram_tensor("spill", [B, P, 2 * CP], F32).ap()

    with ExitStack() as ctx:
        def sb(name, shape, dt=F32):
            return ctx.enter_context(nc.sbuf_tensor(name, shape, dt))

        def sem(name):
            return ctx.enter_context(nc.semaphore(name))

        scores = ctx.enter_context(nc.psum_tensor("scores", [P, 2, 1024], F32))
        turned = ctx.enter_context(nc.psum_tensor("turned", [P, 2, 512], F32))
        spare = ctx.enter_context(nc.psum_tensor("spare", [P, 2, 512], F32))

        mat = sb("mat", [P, NM, P])
        col = sb("col", [P, NCOL])
        row = sb("row", [P, NROW, D])
        ident = sb("ident", [P, P])
        wq1, wk1, wv1, wo1, wq2, wk2, wv2, wo2, wa, wn = (mat[:, i, :] for i in range(10))
        mdct = [mat[:, 10, :], mat[:, 11, :]]
        bq1, bk1, bo1, bq2, bk2, ln_g, ln_b, battn = (col[:, i:i + 1] for i in range(8))
        bv1_row, bv2_row, bo2_row, gamma_row, beta_row, next_row = (row[:, i, :] for i in range(6))
        wf = sb("wf", [P, 3, P])
        wg = sb("wg", [P, P])
        fcol = sb("fcol", [P, 5])
        bo1_wide = sb("bo1_wide", [P, P])
        half_neg = sb("half_neg", [P, NT])

        xt = sb("xt", [P, C + 1])
        hx = sb("hx", [P, 2, CP])
        hxp = sb("hxp", [P, 2, CP])
        hraw = sb("hraw", [P, NT, D])
        x1 = sb("x1", [P, NT, D])
        x1T = sb("x1T", [P, CP])
        hi = sb("hi", [P, 2, C], F32R)
        lo = sb("lo", [P, 2, C], F32R)
        stack = [sb(f"stack{a}", [3 * DK, 2, H, C], F32R) for a in (1, 2)]
        val = [sb(f"val{a}", [P, NT, D]) for a in (1, 2)]
        top = sb("top", [P, 2, 8])
        nbias = sb("nbias", [P, 2])
        expd = sb("expd", [P, 2, C])
        prob = sb("prob", [P, 2, CP])
        rsum = sb("rsum", [P, TILES])
        rinv = sb("rinv", [P, TILES])
        rwide = sb("rwide", [P, 3 * H, DK])
        probT = [sb(f"probT{n}", [P, H, NT, HALF[n][1]]) for n in (0, 1)]
        spread = sb("spread", [P, HALF[0][1]])
        attnT = [sb(f"attnT{a}", [P, C]) for a in (1, 2)]
        hh = sb("hh", [P, NT, D])
        h2 = sb("h2", [P, NT, D])
        h2_old = sb("h2_old", [P, NT, D])
        xf = sb("xf", [P, NT, D])
        nrm = sb("nrm", [P, NT, D])
        nrmT = sb("nrmT", [P, CP])
        xaT = sb("xaT", [P, C])
        expert = sb("expert", [P, experts.shape[2]])
        gT = sb("gT", [P, KH, C])
        yT = sb("yT", [P, C])
        z = sb("z", [P, NT, D])
        gz = sb("gz", [P, NT, D])
        stat = sb("stat", [P, 3, NT, 6])
        mv = sb("mv", [P, 3, NT, 2])
        ve = sb("ve", [P, 3, NT])
        rstd = sb("rstd", [P, 3, NT])
        negm = sb("negm", [P, 3, NT])
        shift = sb("shift", [P, 3, NT])
        var_x = sb("var_x", [P, 2, NT])
        rstd_x = sb("rstd_x", [P, NT])

        consts_in = sem("consts_in")
        prep_v, prep_p, prep_g = sem("prep_v"), sem("prep_p"), sem("prep_g")
        x_in = sem("x_in")
        spill_out, spill_in = sem("spill_out"), sem("spill_in")
        stacked = [sem("stacked1"), sem("stacked2")]
        expert_in = sem("expert_in")
        h2_kept = sem("h2_kept")
        stored = sem("stored")
        spare_full = [sem("spare_full0"), sem("spare_full1")]
        spare_free = [sem("spare_free0"), sem("spare_free1")]
        scores_full = sem("scores_full")
        top_found = sem("top_found")
        bias_ready = sem("bias_ready")
        exp_done = sem("exp_done")
        probs_ready = [sem("probs_ready0"), sem("probs_ready1")]
        turned_full = sem("turned_full")
        turned_free = [sem("turned_free0"), sem("turned_free1")]
        inverse_found = sem("inverse_found")
        wide_ready = sem("wide_ready")
        stats_part = [sem(f"stats_part{n}") for n in range(3)]
        stats_ready = [sem(f"stats_ready{n}") for n in range(3)]
        passed = sem("passed")
        norm_step = [sem(f"norm_step{n}") for n in range(3)]
        x1_ready = sem("x1_ready")
        hx_ready = sem("hx_ready")
        hi_ready = [sem("hi_ready1"), sem("hi_ready2")]
        h2_ready = sem("h2_ready")
        nrm_ready = sem("nrm_ready")
        hidden_ready = sem("hidden_ready")
        gz_ready = sem("gz_ready")
        out_ready = sem("out_ready")

        def batch(it, offset, per, k):
            return it.at(lambda j: (j + offset) * per + k)

        def alone(engine, s, value):
            engine.wait_ge(s, value)
            engine.sem_inc(passed, 1)

        def done(engine, it, offset, *units, bank=None):
            counts = dict(plan.unit_count(it, offset, *unit) for unit in units)
            for b, count in counts.items():
                if b != bank:
                    engine.wait_ge(spare_free[b], count)

        def computed(engine, it, offset, name, part):
            bank, count = plan.unit_count(it, offset, name, part)
            engine.wait_ge(spare_full[bank], count)

        def attention(phase, part):
            return (phase, 0) if part == 0 else ((0, 0) if phase == 1 else (1, 1))

        def attention_count(it, phase, part, per, k):
            phase, back = attention(phase, part)
            return it.at(lambda j: per * plan.phases_before(j - back, phase) + k)

        def half_before(it, off, a, part):
            found = {(0, 0): [(("pv2", 1), -2), (("pv1", 1), -1)], (0, 1): [(("pv1", 0), 0)],
                     (1, 0): [(("pv1", 1), 1), (("pv2", 1), -1)], (1, 1): [(("pv2", 0), 0)]}[a, part]
            return next(((u, off + d) for u, d in found if plan.has(it, off + d)), None)

        def product_before(it, off, a, half):
            found = (("pv2", -2), ("pv1", -1)) if a == 0 else (("pv1", 1), ("pv2", -1))
            return next(((u, off + d) for u, d in found if plan.has(it, off + d)), None)

        def copy_block(engine, copy, it, tile, part):
            phase, off, k, back = tile
            t, h = divmod(k, H)
            m = rows(t)
            n = plan.number(it, tile)
            half = 0 if t in HALF_TILES[0] else 1
            at = t * P - HALF[half][0]
            if t == HALF_TILES[half][0] and h == 0:
                before = product_before(it, off, phase, half)
                if before:
                    computed(engine, it, before[1], before[0], half)
            engine.wait_ge(turned_full, 2 * n + part + 1)
            blocks = ((0, 3), (3, 5))[part]
            src = turned[:, part, 0:(blocks[1] - blocks[0]) * P].rearrange("p (j c) -> p j c", c=P)[:, :, 0:m]
            copy(probT[half][:, h, blocks[0]:blocks[1], at:at + m], src).then_inc(turned_free[part], 1)

        def iterations(engine, body):
            for j in range(-1, plan.loop[0]):
                body(Iteration(j))
            with engine.Fori(*plan.loop) as i:
                body(Iteration(i, plan.loop[0]))
            for j in range(plan.loop[1], B + 3):
                body(Iteration(j))

        block = ctx.enter_context(nc.Block())

        @block.sync
        def _(sp):
            sp.dma_start(mat[:], mats).then_inc(consts_in, 16)
            sp.dma_start(col[:], cols).then_inc(consts_in, 16)
            sp.dma_start(row[:], rows_in.unsqueeze(0).broadcast_to((P, NROW, D))).then_inc(consts_in, 16)
            sp.dma_start(xt[:], xT[0]).then_inc(x_in, 16)

            def done_alone(sp, it, offset, *units):
                for unit in units:
                    done(sp, it, offset, unit)
                    sp.sem_inc(passed, 1)

            def send_stacks(it, a, offset):
                alone(sp, hi_ready[a], batch(it, offset, 4, 4))
                done_alone(sp, it, offset, *[(w + "12"[a], p) for w in "qk" for p in (0, 1)])
                for which, parts in ((0, (hi, hi, lo)), (1, (hi, lo, hi))):
                    for s, part in enumerate(parts):
                        for h in range(H):
                            sp.dma_start(
                                stack[a][s * DK:(s + 1) * DK, which, h, :].bitcast(F32),
                                part[h * DK:(h + 1) * DK, which, :].bitcast(F32),
                            ).then_inc(stacked[a], 16)

            def body(it):
                if plan.has(it, -2):
                    if it.looped or it.like - 3 >= 0:
                        done_alone(sp, it, -3, ("down", 0), ("down", 1))
                    which = (it.index - 2) // 2
                    sp.dma_start(expert[:], experts[which]).then_inc(expert_in, 16)
                if plan.has(it, 2):
                    computed(sp, it, 1, "mdct", 1)
                    sp.sem_inc(passed, 1)
                    sp.dma_start(xt[:], xT[it.index + 2]).then_inc(x_in, 16)
                if plan.has(it, -1):
                    send_stacks(it, 1, -1)
                if plan.has(it, 1):
                    alone(sp, hx_ready, batch(it, 1, 2, 2))
                    sp.dma_start(spill[it.index + 1], hx[:].rearrange("p a c -> p (a c)")).then_inc(spill_out, 16)
                if plan.has(it, 1):
                    send_stacks(it, 0, 1)
                if plan.has(it, -3):
                    alone(sp, out_ready, batch(it, -3, 1, 1))
                    full = (NT - 1) * P
                    dst = out[it.index - 3]
                    sp.dma_start(dst[0:full].rearrange("(t p) f -> p t f", p=P), gz[:, 0:NT - 1, :]).then_inc(stored, 16)
                    sp.dma_start(dst[full:C], gz[0:C - full, NT - 1, :]).then_inc(stored, 16)
                if plan.has(it, -2):
                    if it.looped or it.like - 3 >= 0:
                        alone(sp, out_ready, batch(it, -3, 1, 1))
                    alone(sp, h2_ready, batch(it, -2, 1, 1))
                    sp.dma_start(h2_old[:], h2[:]).then_inc(h2_kept, 16)
                if plan.has(it, -1):
                    if it.looped or it.like - 2 >= 0:
                        alone(sp, h2_ready, batch(it, -2, 1, 1))
                    alone(sp, spill_out, batch(it, -1, 16, 16))
                    sp.dma_start(hxp[:].rearrange("p a c -> p (a c)"), spill[it.index - 1]).then_inc(spill_in, 16)

            iterations(sp, body)
            sp.wait_ge(stored, 32 * B)

        @block.tensor
        def _(pe):
            pe.wait_ge(prep_v, 6)
            pe.wait_ge(consts_in, 48)
            for n, w in enumerate((wq2, wk2, wv2)):
                pe.matmul(spare[:, 0, n * P:(n + 1) * P], wo1, w, start=True, stop=True)
            pe.matmul(spare[:, 1, 0:1], wq2, bo1, start=True, stop=True)
            pe.matmul(spare[:, 1, 1:2], wk2, bo1, start=True, stop=True)
            pe.matmul(spare[:, 1, 2:3], wa, ln_b, start=True, stop=True)
            pe.matmul(spare[:, 1, P:2 * P], bo1_wide[:], wv2, start=True, stop=True).then_inc(prep_p, 1)
            pe.wait_ge(prep_v, 13)
            pe.wait_ge(prep_g, 4)

            def score(it, tile):
                phase, off, k, _ = tile
                t, h = divmod(k, H)
                n = plan.number(it, tile)
                if k == 0:
                    pe.wait_ge(stacked[phase], batch(it, off, 384, 384))
                if it.looped or n >= 2:
                    pe.wait_ge(probs_ready[k % 2], it.at(lambda j: (TILES * plan.phases_before(j - tile[3], phase) + k) // 2))
                m = rows(t)
                q = stack[phase][:, 0, h, t * P:t * P + m]
                kk = stack[phase][:, 1, h, :]
                pe.matmul(scores[0:m, k % 2, S0:S1], q, kk[:, 0:N0], start=True, stop=True)
                pe.matmul(scores[0:m, k % 2, S1:S0 + C], q, kk[:, N0:C], start=True, stop=True).then_inc(scores_full, 1)

            def turn(it, tile):
                phase, off, k, back = tile
                m = rows(k // H)
                n = plan.number(it, tile)
                pe.wait_ge(probs_ready[k % 2], it.at(lambda j: (TILES * plan.phases_before(j - back, phase) + k) // 2 + 1))
                for part, blocks in enumerate(((0, 1, 2), (3, 4))):
                    if it.looped or n >= 1:
                        pe.wait_ge(turned_free[part], n)
                    for b, j in enumerate(blocks):
                        mm = pe.transpose(turned[:, part, b * P:b * P + m], prob[0:m, k % 2, j * P:(j + 1) * P], ident[0:m, 0:m])
                    mm.then_inc(turned_full, 1)

            def values(it, phase, slot, n, u, j):
                name, _, part = u
                bank, _, _ = plan.bank(it, phase, slot, n)
                v, n_c = val[int(name[-1]) - 1], HALF[part][1]
                for h in range(H):
                    mm = pe.matmul(spare[h * DK:(h + 1) * DK, bank, 0:n_c], v[:, j, h * DK:(h + 1) * DK], probT[part][:, h, j, :],
                                   start=(j == 0), stop=(j == NT - 1))
                if j == NT - 1:
                    mm.then_inc(spare_full[bank], 1)

            def unit(it, phase, slot, n, u):
                name, off, part = u
                bank, used, fresh = plan.bank(it, phase, slot, n)
                if it.looped or not fresh:
                    pe.wait_ge(spare_free[bank], used)
                o = spare[:, bank, :]
                lo_c, n_c = HALF[part] if part < 2 else (0, 0)
                a = 0 if name.endswith("1") else 1
                if name == "mdct":
                    if part == 0:
                        pe.wait_ge(x_in, batch(it, off, 16, 16))
                    for t in ((0, 1, 2, 3), (4,))[part]:
                        for c in (0, 1):
                            mm = pe.matmul(o[0:rows(t), (t % 4) * P:(t % 4 + 1) * P], xt[:, t * P + c:t * P + c + rows(t)],
                                           mdct[c], start=(c == 0), stop=(c == 1))
                elif name == "turn":
                    pe.wait_ge(x1_ready, batch(it, off, NT, NT))
                    for t in ((0, 1, 2, 3), (4,))[part]:
                        mm = pe.transpose(o[:, (t % 4) * P:(t % 4 + 1) * P], x1[:, t, :], ident[:])
                elif name == "turn_n":
                    pe.wait_ge(nrm_ready, batch(it, off, NT, NT))
                    for t in ((0, 1, 2, 3), (4,))[part]:
                        mm = pe.transpose(o[:, (t % 4) * P:(t % 4 + 1) * P], nrm[:, t, :], ident[:])
                elif name[0] in "qk":
                    if a == 0:
                        done(pe, it, off, ("turn", 0), ("turn", 1), bank=bank)
                        src, w = x1T, (wq1 if name[0] == "q" else wk1)
                    else:
                        done(pe, it, off, ("pv1", 0), ("pv1", 1), bank=bank)
                        src, w = attnT[0], wf[:, 0 if name[0] == "q" else 1, :]
                    mm = pe.matmul(o[:, 0:n_c], w, src[:, lo_c:lo_c + n_c], start=True, stop=True)
                elif name[0] == "v":
                    src, w = (x1T, wv1) if a == 0 else (attnT[0], wf[:, 2, :])
                    for t in ((0, 1, 2, 3), (4,))[part]:
                        mm = pe.matmul(o[0:rows(t), (t % 4) * P:(t % 4 + 1) * P], src[:, t * P:t * P + rows(t)], w, start=True, stop=True)
                elif name in ("spread1", "spread2"):
                    pe.wait_ge(wide_ready, attention_count(it, phase, part, 3, (1, 3)[part]))
                    for i, t in enumerate(HALF_TILES[part]):
                        m = rows(t)
                        mm = pe.matmul(o[:, i * P:i * P + m], rwide[0:m, i * H:(i + 1) * H, :].rearrange("p h d -> p (h d)"), ident[0:m, 0:m],
                                       start=True, stop=True)
                elif name in ("pv1", "pv2"):
                    last = (HALF_TILES[part][-1] + 1) * H
                    nn = attention_count(it, phase, part, TILES, last)
                    pe.wait_ge(turned_free[0], nn)
                    pe.wait_ge(turned_free[1], nn)
                    if part == 0:
                        done(pe, it, off, ("v" + name[-1], 0), ("v" + name[-1], 1), bank=bank)
                    values(it, phase, slot, n, u, 0)
                    return
                elif name == "wo2":
                    done(pe, it, off, ("pv2", 0), ("pv2", 1), bank=bank)
                    for t in ((0, 1, 2, 3), (4,))[part]:
                        mm = pe.matmul(o[0:rows(t), (t % 4) * P:(t % 4 + 1) * P], attnT[1][:, t * P:t * P + rows(t)], wo2, start=True, stop=True)
                elif name == "mix":
                    done(pe, it, off, ("turn_n", 0), ("turn_n", 1), bank=bank)
                    pe.matmul(o[:, 0:n_c], wg[:], nrmT[:, lo_c:lo_c + n_c], start=True, stop=False)
                    for i, t in enumerate(HALF_TILES[part]):
                        m = rows(t)
                        mm = pe.matmul(o[:, i * P:i * P + m], xf[0:m, t, :], ident[0:m, 0:m], start=False, stop=(t == HALF_TILES[part][-1]))
                elif name == "up":
                    k, half = part % KH, part // KH
                    lo_c, n_c = HALF[half]
                    if k == 0:
                        done(pe, it, off, ("mix", half), bank=bank)
                    if part == 0:
                        pe.wait_ge(expert_in, batch(it, off, 16, 16))
                    mm = pe.matmul(o[:, 0:n_c], expert[:, k * P:(k + 1) * P], xaT[:, lo_c:lo_c + n_c], start=True, stop=True)
                elif name == "down":
                    pe.wait_ge(hidden_ready, batch(it, off, 1, 1))
                    for k in range(KH):
                        mm = pe.matmul(o[:, 0:n_c], expert[:, HID + k * D:HID + (k + 1) * D], gT[:, k, lo_c:lo_c + n_c],
                                       start=(k == 0), stop=(k == KH - 1))
                elif name == "next":
                    done(pe, it, off, ("down", 0), ("down", 1), bank=bank)
                    for t in ((0, 1, 2, 3), (4,))[part]:
                        mm = pe.matmul(o[0:rows(t), (t % 4) * P:(t % 4 + 1) * P], yT[:, t * P:t * P + rows(t)], wn, start=True, stop=True)
                mm.then_inc(spare_full[bank], 1)

            def body(it):
                for phase in (X, Y):
                    for slot in range(TILES):
                        tile = plan.tile(it, phase, slot)
                        if tile:
                            score(it, tile)
                        tile = plan.tile(it, phase, slot, LAG)
                        if tile:
                            turn(it, tile)
                        for n, u in enumerate(plan.slot_units(it, phase, slot)):
                            unit(it, phase, slot, n, u)
                        for block in range(1, NT):
                            for n, u in enumerate(plan.slot_units(it, phase, slot - block)):
                                if u[0][:2] == "pv":
                                    values(it, phase, slot - block, n, u, block)

            iterations(pe, body)

        @block.scalar
        def _(act):
            def exponent(it, tile):
                phase, off, k, back = tile
                m = rows(k // H)
                n = plan.number(it, tile)
                act.wait_ge(bias_ready, n + 1)
                src = scores[0:m, k % 2, S0:S0 + C]
                bias = nbias[0:m, k % 2:k % 2 + 1]
                if phase == 0:
                    act.activation(expd[0:m, k % 2, :], src, ACT.Exp, bias=bias).then_inc(exp_done, 1)
                else:
                    if it.looped or n >= 2:
                        act.wait_ge(turned_full, 2 * n - 2)
                    act.activation(prob[0:m, k % 2, 0:C], src, ACT.Exp, bias=bias,
                                   accum_out=rsum[0:m, k:k + 1]).then_inc(probs_ready[k % 2], 1)

            def unit(it, phase, slot, n, u):
                name, off, part = u
                if name not in ("mdct", "turn", "q1", "k1", "q2", "k2", "spread1", "spread2", "mix"):
                    return
                bank, used, _ = plan.bank(it, phase, slot, n)
                a = 0 if name.endswith("1") else 1
                o = spare[:, bank, :]
                act.wait_ge(spare_full[bank], used + 1)
                if name == "mdct":
                    if part == 0:
                        if it.looped or it.like + off >= 1:
                            act.wait_ge(hx_ready, batch(it, off, 2, 0))
                        i = act.copy(hraw[:, 0:4, :], o.rearrange("p (t f) -> p t f", t=4))
                    else:
                        i = act.copy(hraw[0:rows(4), 4, :], o[0:rows(4), 0:P])
                    i.then_inc(spare_free[bank], 1)
                elif name == "turn":
                    lo_c, n_c = ((0, 4 * P), (4 * P, P))[part]
                    act.copy(x1T[:, lo_c:lo_c + n_c], o[:, 0:n_c]).then_inc(spare_free[bank], 1)
                elif name[0] in "qk":
                    w = 0 if name[0] == "q" else 1
                    lo_c, n_c = HALF[part]
                    if (w, part) == (0, 0):
                        if a == 1:
                            act.wait_ge(stacked[0], it.at(lambda j: min(j + 1, B) * 384))
                        elif it.looped or it.like >= 1:
                            act.wait_ge(stacked[1], it.at(lambda j: j * 384))
                        elif it.like == 0:
                            act.wait_ge(stacked[0], 384)
                    bias = ((fcol[:, 0:1], bk1), (fcol[:, 1:2], fcol[:, 2:3]))[a][w]
                    act.activation(hi[:, w, lo_c:lo_c + n_c], o[:, 0:n_c], ACT.Identity, bias=bias).then_inc(hi_ready[a], 1)
                elif name in ("spread1", "spread2"):
                    n_c = HALF[part][1]
                    before = half_before(it, off, a, part)
                    if before:
                        done(act, it, before[1], before[0])
                    act.copy(spread[:, 0:n_c], o[:, 0:n_c]).then_inc(spare_free[bank], 1)
                elif name == "mix":
                    lo_c, n_c = HALF[part]
                    act.activation(xaT[:, lo_c:lo_c + n_c], o[:, 0:n_c], ACT.Identity, bias=fcol[:, 3:4]).then_inc(spare_free[bank], 1)

            def copy_out(it, tile):
                phase, off, k, back = tile
                for part in ((0, 1) if phase == 0 else (1,)):
                    copy_block(act, act.copy, it, tile, part)

            def body(it):
                for phase in (X, Y):
                    for slot in range(TILES):
                        tile = plan.tile(it, phase, slot)
                        if tile:
                            exponent(it, tile)
                        tile = plan.tile(it, phase, slot, LAG)
                        if tile:
                            copy_out(it, tile)
                        for name, off, _ in plan.JOBS[phase].get(slot, []):
                            if name == "gelu_out" and plan.has(it, off):
                                done(act, it, off, ("next", 0), ("next", 1))
                                if it.looped or it.like + off >= 1:
                                    act.wait_ge(stored, batch(it, off, 32, 0))
                                act.activation(gz[:], z[:], ACT.Gelu).then_inc(gz_ready, 1)
                            if name == "gelu_up" and plan.has(it, off):
                                done(act, it, off, ("up", 2 * KH - 2), ("up", 2 * KH - 1))
                                act.activation(gT[:], gT[:], ACT.Gelu).then_inc(hidden_ready, 1)
                        for place, n, u in plan.results(it, phase, slot):
                            unit(it, phase, place, n, u)

            act.wait_ge(prep_v, 13)
            iterations(act, body)

        @block.vector
        def _(dve):
            for n, buf in enumerate((val[0], val[1], hraw, hh, z)):
                dve.memset(buf[:, NT - 1, :], 0.0).then_inc(prep_v, 1)
            dve.wait_ge(consts_in, 48)
            dve.tensor_copy(bo1_wide[:], bo1.broadcast_to((P, P))).then_inc(prep_v, 1)
            dve.wait_ge(prep_p, 1)
            dve.tensor_scalar(wf[:, 0, :], spare[:, 0, 0:P], SCALE, None, ALU.mult).then_inc(prep_v, 1)
            dve.tensor_copy(wf[:, 1:3, :], spare[:, 0, P:3 * P].rearrange("p (n f) -> p n f", n=2)).then_inc(prep_v, 1)
            dve.tensor_scalar(wg[:], wa, ln_g, None, ALU.mult).then_inc(prep_v, 1)
            dve.tensor_scalar(wq1, wq1, SCALE, None, ALU.mult).then_inc(prep_v, 1)
            dve.tensor_scalar(fcol[:, 0:1], bq1, SCALE, None, ALU.mult).then_inc(prep_v, 1)
            dve.tensor_scalar(fcol[:, 1:2], spare[:, 1, 0:1], bq2, SCALE, ALU.add, ALU.mult).then_inc(prep_v, 1)
            dve.tensor_tensor(fcol[:, 2:3], spare[:, 1, 1:2], bk2, ALU.add)
            dve.tensor_tensor(fcol[:, 3:4], spare[:, 1, 2:3], battn, ALU.add)
            dve.tensor_tensor(bv2_row, spare[:, 1, P:2 * P], bv2_row, ALU.add).then_inc(prep_v, 1)
            dve.wait_ge(prep_v, 13)

            def maximum(it, tile):
                phase, off, k, back = tile
                m = rows(k // H)
                n = plan.number(it, tile)
                src = scores[0:m, k % 2, S0:S0 + C]
                if phase == 0:
                    alone(dve, scores_full, n + 1)
                    dve.max(top[0:m, k % 2, :], src).then_inc(top_found, 1)
                    dve.wait_ge(top_found, batch(it, off, TILES, k + 1))
                    dve.tensor_scalar(nbias[0:m, k % 2:k % 2 + 1], top[0:m, k % 2, 0:1], -1.0, None, ALU.mult).then_inc(bias_ready, 1)
                else:
                    dve.wait_ge(scores_full, n + 1)
                    dve.tensor_reduce(nbias[0:m, k % 2:k % 2 + 1], src, AX.X, ALU.max, negate=True).then_inc(bias_ready, 1)

            def mask(it, tile):
                phase, off, k, back = tile
                if phase == 1:
                    return
                m = rows(k // H)
                n = plan.number(it, tile)
                if it.looped or n >= 2:
                    dve.wait_ge(turned_full, 2 * n - 2)
                dve.wait_ge(exp_done, batch(it, off, TILES, k + 1))
                dve.scalar_tensor_tensor(prob[0:m, k % 2, 0:C], scores[0:m, k % 2, S0:S0 + C], top[0:m, k % 2, TOPK - 1:TOPK],
                                         expd[0:m, k % 2, :], ALU.is_ge, ALU.mult,
                                         accum_out=rsum[0:m, k:k + 1]).then_inc(probs_ready[k % 2], 1)

            def copy_out(it, tile):
                if tile[0] == 1:
                    copy_block(dve, dve.tensor_copy, it, tile, 0)

            def job(it, phase, slot, name, off, part):
                if name in ("inverse1", "inverse2"):
                    a = 0 if name == "inverse1" else 1
                    tiles = HALF_TILES[part]
                    k0, k1 = tiles[0] * H, (tiles[-1] + 1) * H
                    for par in (0, 1):
                        dve.wait_ge(probs_ready[par], attention_count(it, phase, part, TILES // 2, k1 // 2))
                    groups = ((0, 3),) if part == 0 else ((3, 4), (4, 5))
                    for t0, t1 in groups:
                        m = rows(t0)
                        dve.reciprocal(rinv[0:m, t0 * H:t1 * H], rsum[0:m, t0 * H:t1 * H]).then_inc(inverse_found, 1)
                    before = half_before(it, off, a, part)
                    if before:
                        computed(dve, it, before[1], before[0][0].replace("pv", "spread"), before[0][1])
                    dve.wait_ge(inverse_found, attention_count(it, phase, part, 3, (1, 3)[part]))
                    for t0, t1 in groups:
                        m, at = rows(t0), (t0 - tiles[0]) * H
                        dve.tensor_copy(rwide[0:m, at:at + (t1 - t0) * H, :],
                                        rinv[0:m, t0 * H:t1 * H].unsqueeze(2).broadcast_to((m, (t1 - t0) * H, DK))).then_inc(wide_ready, 1)
                elif name in ("stats_h", "stats_hh", "stats_h2"):
                    s, buf = {"stats_h": (0, hraw), "stats_hh": (1, hh), "stats_h2": (2, h2)}[name]
                    if s == 0:
                        done(dve, it, off, ("mdct", 0), ("mdct", 1))
                    elif s == 1:
                        done(dve, it, off, ("wo2", 0), ("wo2", 1))
                    else:
                        dve.wait_ge(h2_ready, batch(it, off, 1, 1))
                    for t in range(NT):
                        dve.bn_stats(stat[:, s, t, :], buf[:, t, :]).then_inc(stats_part[s], 1)
                    alone(dve, stats_part[s], batch(it, off, NT, NT))
                    for t in range(NT):
                        dve.bn_aggr(mv[:, s, t, :], stat[:, s, t, :]).then_inc(stats_ready[s], 1)

            def unit(it, phase, slot, n, u):
                name, off, part = u
                if name not in ("q1", "k1", "q2", "k2", "v1", "v2", "pv1", "pv2", "wo2", "turn_n", "up", "down", "next"):
                    return
                bank, used, _ = plan.bank(it, phase, slot, n)
                a = 0 if name.endswith("1") else 1
                o = spare[:, bank, :]
                tiles = ((0, 4), (4, 5))[part % 2]
                m = rows(tiles[0])
                nt = tiles[1] - tiles[0]
                natural = o[0:m, 0:nt * P].rearrange("p (t f) -> p t f", t=nt)
                dve.wait_ge(spare_full[bank], used + 1)
                if name[0] in "qk":
                    w = 0 if name[0] == "q" else 1
                    lo_c, n_c = HALF[part]
                    bias = ((fcol[:, 0:1], bk1), (fcol[:, 1:2], fcol[:, 2:3]))[a][w]
                    dve.wait_ge(hi_ready[a], batch(it, off, 4, 2 * w + part + 1))
                    i = dve.scalar_tensor_tensor(lo[:, w, lo_c:lo_c + n_c], o[:, 0:n_c], bias, hi[:, w, lo_c:lo_c + n_c].bitcast(F32),
                                                 ALU.add, ALU.subtract)
                elif name[0] == "v":
                    brow = (bv1_row, bv2_row)[a]
                    i = dve.tensor_tensor(val[a][0:m, tiles[0]:tiles[1], :], natural,
                                          brow[0:m].unsqueeze(1).broadcast_to((m, nt, D)), ALU.add)
                elif name in ("pv1", "pv2"):
                    lo_c, n_c = HALF[part]
                    done(dve, it, off, ("spread" + name[-1], part))
                    dve.tensor_tensor(attnT[a][:, lo_c:lo_c + n_c], o[:, 0:n_c], spread[:, 0:n_c], ALU.mult).then_inc(spare_free[bank], 1)
                    return
                elif name == "wo2":
                    if part == 0:
                        dve.wait_ge(spill_in, batch(it, off, 16, 16))
                    xb = hxp[:, 1, :].rearrange("p (t f) -> p t f", t=NT)
                    i = dve.tensor_tensor(hh[0:m, tiles[0]:tiles[1], :], natural, xb[0:m, tiles[0]:tiles[1], :], ALU.add)
                elif name == "turn_n":
                    lo_c, n_c = ((0, 4 * P), (4 * P, P))[part]
                    i = dve.tensor_copy(nrmT[:, lo_c:lo_c + n_c], o[:, 0:n_c])
                elif name == "up":
                    k, half = part % KH, part // KH
                    lo_c, n_c = HALF[half]
                    if part == 0:
                        dve.wait_ge(expert_in, batch(it, off, 16, 16))
                    i = dve.tensor_scalar(gT[:, k, lo_c:lo_c + n_c], o[:, 0:n_c], expert[:, 2 * HID + k:2 * HID + k + 1], None, ALU.add)
                elif name == "down":
                    lo_c, n_c = HALF[part]
                    i = dve.tensor_scalar(yT[:, lo_c:lo_c + n_c], o[:, 0:n_c], expert[:, 2 * HID + KH:2 * HID + KH + 1], None, ALU.add)
                elif name == "next":
                    if part == 0 and (it.looped or it.like + off >= 1):
                        dve.wait_ge(gz_ready, batch(it, off, 1, 0))
                    i = dve.tensor_tensor(z[0:m, tiles[0]:tiles[1], :], natural,
                                          next_row[0:m].unsqueeze(1).broadcast_to((m, nt, D)), ALU.add)
                i.then_inc(spare_free[bank], 1)

            def body(it):
                for phase in (X, Y):
                    for slot in range(TILES):
                        tile = plan.tile(it, phase, slot)
                        if tile:
                            maximum(it, tile)
                        for lag in ((1, 0) if slot % 2 else ()):
                            tile = plan.tile(it, phase, slot, lag)
                            if tile:
                                mask(it, tile)
                        tile = plan.tile(it, phase, slot, LAG)
                        if tile:
                            copy_out(it, tile)
                        for name, off, part in plan.JOBS[phase].get(slot, []):
                            if name[:4] != "gelu" and plan.has(it, off):
                                job(it, phase, slot, name, off, part)
                        for place, n, u in plan.results(it, phase, slot):
                            unit(it, phase, place, n, u)

            iterations(dve, body)

        @block.gpsimd
        def _(pool):
            pool.memset(ident[:], 0.0).then_inc(prep_g, 1)
            pool.memset(half_neg[:], -0.5).then_inc(prep_g, 1)
            pool.memset(prob[:, :, C:CP], 0.0).then_inc(prep_g, 1)
            pool.wait_ge(prep_g, 3)
            pool.affine_select(out=ident[:], in_=ident[:], compare_op=ALU.not_equal, fill=1.0, base=0,
                               pattern=[[-1, P]], channel_multiplier=1).then_inc(prep_g, 1)

            def norm(it, off, s, step, k):
                def before(n):
                    alone(pool, step, batch(it, off, STEPS[s], k + n))
                alone(pool, stats_ready[s], batch(it, off, NT, NT))
                pool.tensor_scalar(ve[:, s, :], mv[:, s, :, 1], EPS, 1.0, ALU.add, ALU.mult).then_inc(step, 1)
                before(1)
                pool.tensor_tensor(rstd[:, s, :], ve[:, s, :], half_neg[:], ALU.pow).then_inc(step, 1)
                before(2)
                pool.tensor_tensor(negm[:, s, :], mv[:, s, :, 0], rstd[:, s, :], ALU.mult).then_inc(step, 1)
                before(3)
                pool.tensor_scalar(shift[:, s, :], negm[:, s, :], -1.0, 1.0, ALU.mult, ALU.mult).then_inc(step, 1)
                before(4)

            def scaled(dst, src, scale, add, ready):
                for t in range(NT):
                    pool.tensor_scalar(dst[:, t, :], src[:, t, :], scale[:, t:t + 1],
                                       add if isinstance(add, float) else add[:, t:t + 1], ALU.mult, ALU.add).then_inc(ready, 1)

            def wide(r):
                return r.unsqueeze(1).broadcast_to((P, NT, D))

            hx_t = hx[:].rearrange("p a (t f) -> p a t f", t=NT)
            hxp_t = hxp[:].rearrange("p a (t f) -> p a t f", t=NT)

            def front(it, off):
                norm(it, off, 0, norm_step[0], 0)
                if it.looped or it.like + off >= 1:
                    computed(pool, it, off - 1, "turn", 1)
                    pool.sem_inc(passed, 1)
                scaled(x1, hraw, rstd[:, 0, :], shift[:, 0, :], x1_ready)
                if it.looped or it.like + off >= 1:
                    alone(pool, spill_out, batch(it, off, 16, 0))
                pool.tensor_tensor(hx_t[:, 0], hraw[:], wide(beta_row), ALU.add).then_inc(hx_ready, 1)
                pool.wait_ge(x1_ready, batch(it, off, NT, NT))
                pool.tensor_tensor(hx_t[:, 1], x1[:], wide(bo2_row), ALU.add).then_inc(hx_ready, 1)

            def post(it, off):
                norm(it, off, 1, norm_step[1], 0)
                if it.looped or it.like + off >= 1:
                    computed(pool, it, off - 1, "mix", 1)
                    pool.sem_inc(passed, 1)
                scaled(xf, hh, rstd[:, 1, :], shift[:, 1, :], norm_step[1])
                pool.wait_ge(norm_step[1], batch(it, off, STEPS[1], 4 + NT))
                pool.tensor_tensor(xf[:], xf[:], wide(gamma_row), ALU.mult).then_inc(norm_step[1], 1)
                if it.looped or it.like + off >= 1:
                    pool.wait_ge(h2_kept, batch(it, off, 16, 0))
                pool.wait_ge(norm_step[1], batch(it, off, STEPS[1], 5 + NT))
                pool.tensor_tensor(h2[:], xf[:], hxp_t[:, 0], ALU.add).then_inc(h2_ready, 1)

                step = norm_step[2]
                norm(it, off, 2, step, 0)
                pool.tensor_tensor(var_x[:, 0, :], mv[:, 2, :, 1], rstd[:, 2, :], ALU.mult).then_inc(step, 1)
                pool.wait_ge(step, batch(it, off, STEPS[2], 5))
                pool.tensor_tensor(var_x[:, 1, :], var_x[:, 0, :], rstd[:, 2, :], ALU.mult).then_inc(step, 1)
                alone(pool, step, batch(it, off, STEPS[2], 6))
                pool.tensor_scalar(var_x[:, 0, :], var_x[:, 1, :], EPS, 1.0, ALU.add, ALU.mult).then_inc(step, 1)
                pool.wait_ge(step, batch(it, off, STEPS[2], 7))
                pool.tensor_tensor(rstd_x[:], var_x[:, 0, :], half_neg[:], ALU.pow).then_inc(step, 1)
                scaled(xf, h2, rstd[:, 2, :], shift[:, 2, :], step)
                if it.looped or it.like + off >= 1:
                    computed(pool, it, off - 1, "turn_n", 1)
                    pool.sem_inc(passed, 1)
                alone(pool, step, batch(it, off, STEPS[2], 8 + NT))
                scaled(nrm, xf, rstd_x, 0.0, nrm_ready)

            def final(it, off):
                pool.wait_ge(gz_ready, batch(it, off, 1, 1))
                pool.wait_ge(h2_kept, batch(it, off, 16, 16))
                pool.tensor_tensor(gz[:], gz[:], h2_old[:], ALU.add).then_inc(out_ready, 1)

            def body(it):
                if plan.has(it, 1):
                    front(it, 1)
                if plan.has(it, -2):
                    post(it, -2)
                if plan.has(it, -3):
                    final(it, -3)

            pool.wait_ge(consts_in, 48)
            pool.wait_ge(prep_v, 13)
            iterations(pool, body)


def kernel(**inputs):
    import concourse.bacc as bacc
    from concourse.bass_utils import run_bass_kernel_spmd

    arr = {k: np.ascontiguousarray(v) for k, v in inputs.items()}
    attn = {k[len("L0_attn_"):]: v for k, v in arr.items() if k.startswith("L0_attn_")}
    ffn = {k[len("L0_ffn_"):]: v for k, v in arr.items() if k.startswith("L0_ffn_")}
    x = arr["x"]
    batches, samples = x.shape

    blocks = np.zeros((batches, C + 1, P), np.float32)
    blocks.reshape(batches, -1)[:, P:P + samples] = x
    xT = np.ascontiguousarray(blocks.transpose(0, 2, 1))

    length = 2 * P
    n = np.arange(length, dtype=np.float32) + np.float32(0.5)
    k = np.float32(np.pi / P) * n[:P]
    table = np.sqrt(np.float32(4.0 / P)) * np.cos((n + np.float32(P / 2))[:, None] * k[None, :])
    window = np.sin(np.float32(np.pi) * n / np.float32(length))
    mdct = (window[:, None] * table).astype(np.float32)

    mats = np.ascontiguousarray(np.stack(
        [attn["Wq1"].T, attn["Wk1"].T, attn["Wv1"].T, attn["Wo1"], attn["Wq2"].T, attn["Wk2"].T, attn["Wv2"].T,
         attn["Wo2"].T, ffn["attn_w"].T, ffn["next_w"].T, mdct[:P], mdct[P:]], axis=1))
    cols = np.ascontiguousarray(np.stack(
        [attn["bq1"], attn["bk1"], attn["bo1"], attn["bq2"], attn["bk2"], ffn["ln_g"], ffn["ln_b"], ffn["attn_b"]], axis=1))
    rows_in = np.stack([attn["bv1"], attn["bv2"], attn["bo2"], attn["gamma"], attn["beta"], ffn["next_b"]])
    e = ffn["fc1_w"].shape[0]
    experts = np.concatenate(
        [ffn["fc1_w"].transpose(0, 2, 1),
         ffn["fc2_w"].transpose(0, 2, 1).reshape(e, KH, P, D).transpose(0, 2, 1, 3).reshape(e, P, KH * D),
         ffn["fc1_b"].reshape(e, KH, P).transpose(0, 2, 1), ffn["fc2_b"][:, :, None]], axis=2)
    experts = np.ascontiguousarray(np.concatenate([experts, experts]))

    given = {"xT": xT, "mats": mats, "cols": cols, "rows_in": rows_in, "experts": experts}
    nc = bacc.Bacc("TRN2", target_bir_lowering=False, num_devices=1)
    aps = {name: nc.dram_tensor(name, a.shape, F32, kind="ExternalInput").ap() for name, a in given.items()}
    out = nc.dram_tensor("out", (batches, C, D), F32, kind="ExternalOutput").ap()
    build(nc, **aps, out=out)
    result = run_bass_kernel_spmd(nc, [given], core_ids=[0])
    return result.results[0]["out"]
```

```python
from contextlib import ExitStack

import numpy as np

import concourse.bass as bass
from concourse import mybir

F32 = mybir.dt.float32
F32R = mybir.dt.float32r
ALU = mybir.AluOpType
ACT = mybir.ActivationFunctionType
AX = mybir.AxisListType

P = 128
C = 626
D = 128
H = 4
DK = D // H
TOPK = 5
NT = -(-C // P)
CP = NT * P
HID = 512
KH = HID // P
EPS = 1e-5
SCALE = float(DK) ** -0.5
TILES = NT * H
HALF = ((0, 384), (384, C - 384))
HALF_TILES = ((0, 1, 2), (3, 4))
S0, S1 = 198, 512
N0 = S1 - S0
STEPS = (4, 5 + NT, 8 + NT)
PROBS = 4
LAG = 3
LEAD = 1


def rows(t):
    return min(P, C - t * P)


class Iteration:

    def __init__(self, index, first=None):
        self.index, self.looped = index, first is not None
        self.like = first if self.looped else index

    def at(self, f):
        if not self.looped:
            return f(self.index)
        start, step = f(self.like), f(self.like + 1) - f(self.like)
        return self.index * step + (start - step * self.like)


class Plan:

    X, Y = 0, 1

    UNITS = {
        X: {
            0: [("mdct", 1, 0), ("mdct", 1, 1)],
            1: [("v1", 0, 0), ("v1", 0, 1)],
            2: [("k2", -1, 0), ("k2", -1, 1)],
            3: [("spread2", -2, 1), ("pv2", -2, 1)],
            8: [("wo2", -2, 0), ("wo2", -2, 1)],
            9: [("down", -3, 0)],
            10: [("down", -3, 1)],
            11: [("v2", -1, 0), ("v2", -1, 1)],
            12: [("turn", 1, 0), ("turn", 1, 1)],
            13: [("next", -3, 0), ("next", -3, 1)],
            14: [("spread1", 0, 0), ("pv1", 0, 0)],
        },
        Y: {
            0: [("q1", 1, 0), ("q1", 1, 1)],
            1: [("turn_n", -2, 0), ("turn_n", -2, 1)],
            2: [("k1", 1, 0), ("k1", 1, 1)],
            3: [("spread1", 0, 1), ("pv1", 0, 1)],
            8: [("mix", -2, 0), ("mix", -2, 1)],
            9: [("up", -2, 0), ("up", -2, 1)],
            10: [("up", -2, 2), ("up", -2, 3)],
            11: [("q2", 0, 0), ("q2", 0, 1)],
            12: [("up", -2, 4), ("up", -2, 5)],
            13: [("up", -2, 6), ("up", -2, 7)],
            14: [("spread2", -1, 0), ("pv2", -1, 0)],
        },
    }
    BLOCKS = ((0,), (1,), (2,), (3,), (4,))
    TAKER = {"q1": "act", "k1": "act", "q2": "act", "k2": "act", "v1": "act", "v2": "dve", "mdct": "act", "turn": "act",
             "turn_n": "dve", "spread1": "act", "spread2": "dve", "mix": "act", "up": "dve", "down": "act"}
    COPIES = {X: [("act", "act"), ("act", "act"), ("act", "act"), ("act", "act")],
              Y: [("dve", "dve"), ("dve", "dve"), ("dve", "dve"), ("dve", "act")]}
    LATE = {"act": {"spread1": 2}, "dve": {}}
    ORDER = {("pe", X): ("score", "turn", "units"),
             ("pe", Y): ("score", "turn", "units"),
             ("act", X): ("copies", "results", "jobs"),
             ("act", Y): ("copies", "results", "jobs"),
             ("dve", X): ("copies", "results", "jobs"),
             ("dve", Y): ("jobs", "copies", "results")}
    JOBS = {
        X: {2: [("inverse2", -2, 1)], 6: [("stats_h", 1, 0)], 10: [("stats_hh", -2, 0)], 11: [("inverse1", 0, 0)], 16: [("stats_h2", -2, 0)]},
        Y: {1: [("inverse1", 0, 1)], 13: [("gelu_out", -3, 0), ("inverse2", -1, 0)], 15: [("gelu_up", -2, 0)]},
    }

    def __init__(self, batches):
        self.batches = batches
        self.loop = (4, batches - 2)
        self.unit_total = {}

    def has(self, it, offset):
        return it.looped or 0 <= it.like + offset < self.batches

    def phase_exists(self, j, phase):
        return 0 <= j - phase < self.batches

    def phases_before(self, j, phase=0):
        n = sum(self.phase_exists(i, q) for i in range(j) for q in (0, 1))
        return n + (phase == 1 and self.phase_exists(j, 0))

    def tile(self, it, phase, slot, lag=0):
        k, back = slot - lag, 0
        if k < 0:
            k += TILES
            phase, back = (0, 0) if phase == 1 else (1, 1)
        if not it.looped and not self.phase_exists(it.like - back, phase):
            return None
        return phase, -back - phase, k, back

    def number(self, it, tile):
        phase, _, k, back = tile
        return it.at(lambda j: TILES * self.phases_before(j - back, phase) + k)

    def half_number(self, it, phase, back):
        return it.at(lambda j: self.phases_before(j - back, phase))

    def slot_units(self, it, phase, slot):
        return [u for u in self.UNITS[phase].get(slot, []) if self.has(it, u[1])]

    def results(self, it, phase, slot, engine):
        found = []
        for place in range(slot - len(self.BLOCKS) - 1, slot + 1):
            for n, u in enumerate(self.slot_units(it, phase, place)):
                last = len(self.BLOCKS) - 1 if u[0][:2] == "pv" else 0
                if place + last + self.LATE[engine].get(u[0], LEAD) == slot:
                    found.append((place, n, u))
        return found

    def units_before(self, j, phase, slot, n):
        if j not in self.unit_total:
            self.unit_total[j] = sum(self.units_in(i, 2, 0) for i in range(-1, j))
        return self.unit_total[j] + self.units_in(j, phase, slot) + n

    def units_in(self, j, phase, slot):
        return sum(
            0 <= j + u[1] < self.batches
            for q in (0, 1) for s, us in self.UNITS[q].items() if (q, s) < (phase, slot) for u in us
        )

    def bank(self, it, phase, slot, n):
        u = self.units_before(it.like, phase, slot, n)
        return u % 2, it.at(lambda j: self.units_before(j, phase, slot, n) // 2), u < 2

    def place(self, name, part):
        for phase, slots in self.UNITS.items():
            for slot, units in slots.items():
                for n, u in enumerate(units):
                    if (u[0], u[2]) == (name, part):
                        return phase, slot, n, u[1]
        raise KeyError(name)

    def unit_count(self, it, offset, name, part):
        phase, slot, n, own = self.place(name, part)
        back = own - offset

        def number(j):
            present = self.UNITS[phase][slot][:n]
            before = sum(0 <= j + u[1] < self.batches for u in present)
            return self.units_before(j, phase, slot, before)

        u = number(it.like - back)
        return u % 2, it.at(lambda j: number(j - back) // 2 + 1)


def build(nc, xT, mats, cols, rows_in, experts, out):
    B = xT.shape[0]
    plan = Plan(B)
    X, Y = Plan.X, Plan.Y
    NM, NCOL, NROW = mats.shape[1], cols.shape[1], rows_in.shape[0]
    spill = nc.dram_tensor("spill", [B, P, 2 * CP], F32).ap()

    with ExitStack() as ctx:
        def sb(name, shape, dt=F32):
            return ctx.enter_context(nc.sbuf_tensor(name, shape, dt))

        def sem(name):
            return ctx.enter_context(nc.semaphore(name))

        scores = ctx.enter_context(nc.psum_tensor("scores", [P, 2, 1024], F32))
        turned = ctx.enter_context(nc.psum_tensor("turned", [P, 2, 512], F32))
        spare = ctx.enter_context(nc.psum_tensor("spare", [P, 2, 512], F32))

        mat = sb("mat", [P, NM, P])
        col = sb("col", [P, NCOL])
        row = sb("row", [P, NROW, D])
        ident = sb("ident", [P, P])
        wq1, wk1, wv1, wo1, wq2, wk2, wv2, wo2, wa, wn = (mat[:, i, :] for i in range(10))
        wo1_turned = mat[:, 12, :]
        mdct = [mat[:, 10, :], mat[:, 11, :]]
        bq1, bk1, bo1, bq2, bk2, ln_g, ln_b, battn, bv1, bv2 = (col[:, i:i + 1] for i in range(10))
        bo2_row, gamma_row, beta_row, next_row = (row[:, i, :] for i in range(4))
        wf = sb("wf", [P, 3, P])
        wg = sb("wg", [P, P])
        fcol = sb("fcol", [P, 5])
        bv2_wide = sb("bv2_wide", [P, P])
        half_neg = sb("half_neg", [P, NT])

        xt = sb("xt", [P, C + 1])
        hx = sb("hx", [P, 2, CP])
        hxp = sb("hxp", [P, 2, CP])
        hraw = sb("hraw", [P, NT, D])
        x1 = sb("x1", [P, NT, D])
        x1T = sb("x1T", [P, CP])
        hi = sb("hi", [P, 2, C], F32R)
        lo = sb("lo", [P, 2, C], F32R)
        stack = [sb(f"stack{a}", [3 * DK, 2, H, C], F32R) for a in (1, 2)]
        val = [sb(f"val{a}", [P, NT, D]) for a in (1, 2)]
        top = sb("top", [P, 2, 8])
        nbias = sb("nbias", [P, 2])
        expd = sb("expd", [P, 2, C])
        prob = sb("prob", [P, PROBS, CP])
        rsum = sb("rsum", [P, TILES])
        rinv = sb("rinv", [P, TILES])
        rwide = sb("rwide", [P, 3 * H, DK])
        probT = [sb(f"probT{n}", [P, H, NT, HALF[n][1]]) for n in (0, 1)]
        spread = sb("spread", [P, HALF[0][1]])
        attnT = [sb(f"attnT{a}", [P, C]) for a in (1, 2)]
        hh = sb("hh", [P, NT, D])
        h2 = sb("h2", [P, NT, D])
        h2_old = sb("h2_old", [P, NT, D])
        xf = sb("xf", [P, NT, D])
        nrm = sb("nrm", [P, NT, D])
        nrmT = sb("nrmT", [P, CP])
        xaT = sb("xaT", [P, C])
        expert = sb("expert", [P, experts.shape[2]])
        gT = sb("gT", [P, KH, C])
        yT = sb("yT", [P, C])
        z = sb("z", [P, NT, D])
        gz = sb("gz", [P, NT, D])
        stat = sb("stat", [P, 3, NT, 6])
        mv = sb("mv", [P, 3, NT, 2])
        ve = sb("ve", [P, 3, NT])
        rstd = sb("rstd", [P, 3, NT])
        negm = sb("negm", [P, 3, NT])
        shift = sb("shift", [P, 3, NT])
        var_x = sb("var_x", [P, 2, NT])
        rstd_x = sb("rstd_x", [P, NT])

        consts_in = sem("consts_in")
        prep_v, prep_p, prep_g = sem("prep_v"), sem("prep_p"), sem("prep_g")
        x_in = sem("x_in")
        spill_out, spill_in = sem("spill_out"), sem("spill_in")
        stacked = [sem("stacked1"), sem("stacked2")]
        expert_in = sem("expert_in")
        h2_kept = sem("h2_kept")
        stored = sem("stored")
        spare_full = [sem("spare_full0"), sem("spare_full1")]
        spare_free = [sem("spare_free0"), sem("spare_free1")]
        scores_full = sem("scores_full")
        top_found = sem("top_found")
        bias_ready = [sem("bias_ready1"), sem("bias_ready2")]
        exp_done = sem("exp_done")
        probs_ready = [sem("probs_ready0"), sem("probs_ready1")]
        turned_full = sem("turned_full")
        turned_free = [sem("turned_free0"), sem("turned_free1")]
        inverse_found = sem("inverse_found")
        wide_ready = sem("wide_ready")
        stats_part = [sem(f"stats_part{n}") for n in range(3)]
        stats_ready = [sem(f"stats_ready{n}") for n in range(3)]
        passed = sem("passed")
        norm_step = [sem(f"norm_step{n}") for n in range(3)]
        x1_ready = sem("x1_ready")
        hx_ready = sem("hx_ready")
        split = [sem("split1"), sem("split2")]
        h2_ready = sem("h2_ready")
        nrm_ready = sem("nrm_ready")
        hidden_ready = sem("hidden_ready")
        gz_ready = sem("gz_ready")
        out_ready = sem("out_ready")

        def batch(it, offset, per, k):
            return it.at(lambda j: (j + offset) * per + k)

        def alone(engine, s, value):
            engine.wait_ge(s, value)
            engine.sem_inc(passed, 1)

        def done(engine, it, offset, *units, bank=None):
            counts = dict(plan.unit_count(it, offset, *unit) for unit in units)
            for b, count in counts.items():
                if b != bank:
                    engine.wait_ge(spare_free[b], count)

        def computed(engine, it, offset, name, part):
            bank, count = plan.unit_count(it, offset, name, part)
            engine.wait_ge(spare_full[bank], count)

        def attention(phase, part):
            return (phase, 0) if part == 0 else ((0, 0) if phase == 1 else (1, 1))

        def attention_count(it, phase, part, per, k):
            phase, back = attention(phase, part)
            return it.at(lambda j: per * plan.phases_before(j - back, phase) + k)

        def half_before(it, off, a, part):
            found = {(0, 0): [(("pv2", 1), -2), (("pv1", 1), -1)], (0, 1): [(("pv1", 0), 0)],
                     (1, 0): [(("pv1", 1), 1), (("pv2", 1), -1)], (1, 1): [(("pv2", 0), 0)]}[a, part]
            return next(((u, off + d) for u, d in found if plan.has(it, off + d)), None)

        def product_before(it, off, a, half):
            found = (("pv2", -2), ("pv1", -1)) if a == 0 else (("pv1", 1), ("pv2", -1))
            return next(((u, off + d) for u, d in found if plan.has(it, off + d)), None)

        def copy_block(engine, copy, it, tile, part):
            phase, off, k, back = tile
            t, h = divmod(k, H)
            m = rows(t)
            n = plan.number(it, tile)
            half = 0 if t in HALF_TILES[0] else 1
            at = t * P - HALF[half][0]
            if t == HALF_TILES[half][0] and h == 0:
                before = product_before(it, off, phase, half)
                if before:
                    computed(engine, it, before[1], before[0], half)
            engine.wait_ge(turned_full, 2 * n + part + 1)
            blocks = ((0, 3), (3, 5))[part]
            src = turned[:, part, 0:(blocks[1] - blocks[0]) * P].rearrange("p (j c) -> p j c", c=P)[:, :, 0:m]
            copy(probT[half][:, h, blocks[0]:blocks[1], at:at + m], src).then_inc(turned_free[part], 1)

        def take(engine, copy, biased, it, name, off, part, bank):
            o = spare[:, bank, :]
            if name in ("mdct", "turn", "turn_n"):
                lo_c, n_c = ((0, 4 * P), (4 * P, P))[part]
            elif name != "up":
                lo_c, n_c = HALF[part]
            if name == "mdct":
                if part == 0:
                    if it.looped or it.like + off >= 1:
                        engine.wait_ge(hx_ready, batch(it, off, 2, 0))
                    i = copy(hraw[:, 0:4, :], o.rearrange("p (t f) -> p t f", t=4))
                else:
                    i = copy(hraw[0:rows(4), 4, :], o[0:rows(4), 0:P])
            elif name in ("turn", "turn_n"):
                i = copy((x1T if name == "turn" else nrmT)[:, lo_c:lo_c + n_c], o[:, 0:n_c])
            elif name in ("spread1", "spread2"):
                before = half_before(it, off, int(name[-1]) - 1, part)
                if before:
                    done(engine, it, before[1], before[0])
                i = copy(spread[:, 0:n_c], o[:, 0:n_c])
            elif name[0] in "qk":
                a, w = int(name[-1]) - 1, int(name[0] == "k")
                if (w, part) == (0, 0):
                    if a == 1:
                        engine.wait_ge(stacked[0], it.at(lambda j: min(j + off + 2, B) * 384))
                    elif it.looped or it.like + off >= 2:
                        engine.wait_ge(stacked[1], batch(it, off, 384, -384))
                    elif it.like + off == 1:
                        engine.wait_ge(stacked[0], 384)
                bias = ((fcol[:, 0:1], bk1), (fcol[:, 1:2], fcol[:, 2:3]))[a][w]
                i = biased(lo[:, w, lo_c:lo_c + n_c].bitcast(F32), o[:, 0:n_c], bias)
            elif name[0] == "v":
                tiles = ((0, 4), (4, 5))[part]
                m, nt = rows(tiles[0]), tiles[1] - tiles[0]
                i = copy(val[int(name[-1]) - 1][0:m, tiles[0]:tiles[1], :], o[0:m, 0:nt * P].rearrange("p (t f) -> p t f", t=nt))
            elif name == "mix":
                i = biased(xaT[:, lo_c:lo_c + n_c], o[:, 0:n_c], fcol[:, 3:4])
            elif name == "up":
                k, (lo_c, n_c) = part % KH, HALF[part // KH]
                if part == 0:
                    engine.wait_ge(expert_in, batch(it, off, 16, 16))
                i = biased(gT[:, k, lo_c:lo_c + n_c], o[:, 0:n_c], expert[:, 2 * HID + k:2 * HID + k + 1])
            elif name == "down":
                i = biased(yT[:, lo_c:lo_c + n_c], o[:, 0:n_c], expert[:, 2 * HID + KH:2 * HID + KH + 1])
            i.then_inc(spare_free[bank], 1)

        def iterations(engine, body):
            for j in range(-1, plan.loop[0]):
                body(Iteration(j))
            with engine.Fori(*plan.loop) as i:
                body(Iteration(i, plan.loop[0]))
            for j in range(plan.loop[1], B + 3):
                body(Iteration(j))

        block = ctx.enter_context(nc.Block())

        @block.sync
        def _(sp):
            sp.dma_start(mat[:], mats).then_inc(consts_in, 16)
            sp.dma_start(col[:], cols).then_inc(consts_in, 16)
            sp.dma_start(row[:], rows_in.unsqueeze(0).broadcast_to((P, NROW, D))).then_inc(consts_in, 16)
            sp.dma_start(xt[:], xT[0]).then_inc(x_in, 16)

            def done_alone(sp, it, offset, *units):
                for unit in units:
                    done(sp, it, offset, unit)
                    sp.sem_inc(passed, 1)

            def send_stacks(it, a, offset):
                alone(sp, split[a], batch(it, offset, 4, 4))
                for which, parts in ((0, (hi, hi, lo)), (1, (hi, lo, hi))):
                    for s, part in enumerate(parts):
                        for h in range(H):
                            sp.dma_start(
                                stack[a][s * DK:(s + 1) * DK, which, h, :].bitcast(F32),
                                part[h * DK:(h + 1) * DK, which, :].bitcast(F32),
                            ).then_inc(stacked[a], 16)

            def body(it):
                if plan.has(it, -2):
                    if it.looped or it.like - 3 >= 0:
                        done_alone(sp, it, -3, ("down", 0), ("down", 1))
                    which = (it.index - 2) // 2
                    sp.dma_start(expert[:], experts[which]).then_inc(expert_in, 16)
                if plan.has(it, 2):
                    computed(sp, it, 1, "mdct", 1)
                    sp.sem_inc(passed, 1)
                    sp.dma_start(xt[:], xT[it.index + 2]).then_inc(x_in, 16)
                if plan.has(it, -1):
                    send_stacks(it, 1, -1)
                if plan.has(it, 1):
                    alone(sp, hx_ready, batch(it, 1, 2, 2))
                    sp.dma_start(spill[it.index + 1], hx[:].rearrange("p a c -> p (a c)")).then_inc(spill_out, 16)
                if plan.has(it, 1):
                    send_stacks(it, 0, 1)
                if plan.has(it, -3):
                    alone(sp, out_ready, batch(it, -3, 1, 1))
                    full = (NT - 1) * P
                    dst = out[it.index - 3]
                    sp.dma_start(dst[0:full].rearrange("(t p) f -> p t f", p=P), gz[:, 0:NT - 1, :]).then_inc(stored, 16)
                    sp.dma_start(dst[full:C], gz[0:C - full, NT - 1, :]).then_inc(stored, 16)
                if plan.has(it, -2):
                    if it.looped or it.like - 3 >= 0:
                        alone(sp, out_ready, batch(it, -3, 1, 1))
                    alone(sp, h2_ready, batch(it, -2, 1, 1))
                    sp.dma_start(h2_old[:], h2[:]).then_inc(h2_kept, 16)
                if plan.has(it, -1):
                    if it.looped or it.like - 2 >= 0:
                        alone(sp, h2_ready, batch(it, -2, 1, 1))
                    alone(sp, spill_out, batch(it, -1, 16, 16))
                    sp.dma_start(hxp[:].rearrange("p a c -> p (a c)"), spill[it.index - 1]).then_inc(spill_in, 16)

            iterations(sp, body)
            sp.wait_ge(stored, 32 * B)

        @block.tensor
        def _(pe):
            pe.wait_ge(consts_in, 48)
            for n, w in enumerate((wq2, wk2, wv2)):
                pe.matmul(spare[:, 0, n * P:(n + 1) * P], wo1, w, start=True, stop=True)
            pe.matmul(spare[:, 1, 0:1], wa, ln_b, start=True, stop=True)
            pe.matmul(spare[:, 1, 1:2], wo1_turned, bv1, start=True, stop=True).then_inc(prep_p, 1)
            pe.wait_ge(prep_v, 6)
            for n, w in enumerate((wq2, wk2, wv2)):
                mm = pe.matmul(spare[:, 1, 2 + n:3 + n], w, bo1, start=True, stop=True)
            mm.then_inc(prep_p, 1)
            pe.wait_ge(prep_v, 13)
            pe.matmul(spare[:, 1, P:2 * P], bv2_wide[:], wo2, start=True, stop=True).then_inc(prep_p, 1)
            pe.wait_ge(prep_v, 14)
            pe.wait_ge(prep_g, 4)

            def score(it, tile):
                phase, off, k, _ = tile
                t, h = divmod(k, H)
                n = plan.number(it, tile)
                if k == 0:
                    pe.wait_ge(stacked[phase], batch(it, off, 384, 384))
                if it.looped or n >= 2:
                    pe.wait_ge(probs_ready[k % 2], it.at(lambda j: (TILES * plan.phases_before(j - tile[3], phase) + k) // 2))
                m = rows(t)
                q = stack[phase][:, 0, h, t * P:t * P + m]
                kk = stack[phase][:, 1, h, :]
                pe.matmul(scores[0:m, k % 2, S0:S1], q, kk[:, 0:N0], start=True, stop=True)
                pe.matmul(scores[0:m, k % 2, S1:S0 + C], q, kk[:, N0:C], start=True, stop=True).then_inc(scores_full, 1)

            def turn(it, tile):
                phase, off, k, back = tile
                m = rows(k // H)
                n = plan.number(it, tile)
                pe.wait_ge(probs_ready[k % 2], it.at(lambda j: (TILES * plan.phases_before(j - back, phase) + k) // 2 + 1))
                for part, blocks in enumerate(((0, 1, 2), (3, 4))):
                    if it.looped or n >= 1:
                        pe.wait_ge(turned_free[part], n)
                    for b, j in enumerate(blocks):
                        mm = pe.transpose(turned[:, part, b * P:b * P + m], prob[0:m, k % PROBS, j * P:(j + 1) * P], ident[0:m, 0:m])
                    mm.then_inc(turned_full, 1)

            def values(it, phase, slot, n, u, blocks):
                name, _, part = u
                bank, _, _ = plan.bank(it, phase, slot, n)
                v, n_c = val[int(name[-1]) - 1], HALF[part][1]
                for j in blocks:
                    for h in range(H):
                        mm = pe.matmul(spare[h * DK:(h + 1) * DK, bank, 0:n_c], v[:, j, h * DK:(h + 1) * DK], probT[part][:, h, j, :],
                                       start=(j == 0), stop=(j == NT - 1))
                if NT - 1 in blocks:
                    mm.then_inc(spare_full[bank], 1)

            def unit(it, phase, slot, n, u):
                name, off, part = u
                bank, used, fresh = plan.bank(it, phase, slot, n)
                if it.looped or not fresh:
                    pe.wait_ge(spare_free[bank], used)
                o = spare[:, bank, :]
                lo_c, n_c = HALF[part] if part < 2 else (0, 0)
                a = 0 if name.endswith("1") else 1
                if name == "mdct":
                    if part == 0:
                        pe.wait_ge(x_in, batch(it, off, 16, 16))
                    for t in ((0, 1, 2, 3), (4,))[part]:
                        for c in (0, 1):
                            mm = pe.matmul(o[0:rows(t), (t % 4) * P:(t % 4 + 1) * P], xt[:, t * P + c:t * P + c + rows(t)],
                                           mdct[c], start=(c == 0), stop=(c == 1))
                elif name == "turn":
                    pe.wait_ge(x1_ready, batch(it, off, NT, NT))
                    for t in ((0, 1, 2, 3), (4,))[part]:
                        mm = pe.transpose(o[:, (t % 4) * P:(t % 4 + 1) * P], x1[:, t, :], ident[:])
                elif name == "turn_n":
                    pe.wait_ge(nrm_ready, batch(it, off, NT, NT))
                    for t in ((0, 1, 2, 3), (4,))[part]:
                        mm = pe.transpose(o[:, (t % 4) * P:(t % 4 + 1) * P], nrm[:, t, :], ident[:])
                elif name[0] in "qk":
                    if a == 0:
                        done(pe, it, off, ("turn", 0), ("turn", 1), bank=bank)
                        src, w = x1T, (wq1 if name[0] == "q" else wk1)
                    else:
                        done(pe, it, off, ("pv1", 0), ("pv1", 1), bank=bank)
                        src, w = attnT[0], wf[:, 0 if name[0] == "q" else 1, :]
                    mm = pe.matmul(o[:, 0:n_c], w, src[:, lo_c:lo_c + n_c], start=True, stop=True)
                elif name[0] == "v":
                    src, w = (x1T, wv1) if a == 0 else (attnT[0], wf[:, 2, :])
                    for t in ((0, 1, 2, 3), (4,))[part]:
                        mm = pe.matmul(o[0:rows(t), (t % 4) * P:(t % 4 + 1) * P], src[:, t * P:t * P + rows(t)], w, start=True, stop=True)
                elif name in ("spread1", "spread2"):
                    pe.wait_ge(wide_ready, attention_count(it, phase, part, 3, (1, 3)[part]))
                    for i, t in enumerate(HALF_TILES[part]):
                        m = rows(t)
                        mm = pe.matmul(o[:, i * P:i * P + m], rwide[0:m, i * H:(i + 1) * H, :].rearrange("p h d -> p (h d)"), ident[0:m, 0:m],
                                       start=True, stop=True)
                elif name in ("pv1", "pv2"):
                    last = (HALF_TILES[part][-1] + 1) * H
                    nn = attention_count(it, phase, part, TILES, last)
                    pe.wait_ge(turned_free[0], nn)
                    pe.wait_ge(turned_free[1], nn)
                    if part == 0:
                        done(pe, it, off, ("v" + name[-1], 0), ("v" + name[-1], 1), bank=bank)
                    values(it, phase, slot, n, u, plan.BLOCKS[0])
                    return
                elif name == "wo2":
                    done(pe, it, off, ("pv2", 0), ("pv2", 1), bank=bank)
                    for t in ((0, 1, 2, 3), (4,))[part]:
                        mm = pe.matmul(o[0:rows(t), (t % 4) * P:(t % 4 + 1) * P], attnT[1][:, t * P:t * P + rows(t)], wo2, start=True, stop=True)
                elif name == "mix":
                    done(pe, it, off, ("turn_n", 0), ("turn_n", 1), bank=bank)
                    pe.matmul(o[:, 0:n_c], wg[:], nrmT[:, lo_c:lo_c + n_c], start=True, stop=False)
                    for i, t in enumerate(HALF_TILES[part]):
                        m = rows(t)
                        mm = pe.matmul(o[:, i * P:i * P + m], xf[0:m, t, :], ident[0:m, 0:m], start=False, stop=(t == HALF_TILES[part][-1]))
                elif name == "up":
                    k, half = part % KH, part // KH
                    lo_c, n_c = HALF[half]
                    if k == 0:
                        done(pe, it, off, ("mix", half), bank=bank)
                    if part == 0:
                        pe.wait_ge(expert_in, batch(it, off, 16, 16))
                    mm = pe.matmul(o[:, 0:n_c], expert[:, k * P:(k + 1) * P], xaT[:, lo_c:lo_c + n_c], start=True, stop=True)
                elif name == "down":
                    pe.wait_ge(hidden_ready, batch(it, off, 1, 1))
                    for k in range(KH):
                        mm = pe.matmul(o[:, 0:n_c], expert[:, HID + k * D:HID + (k + 1) * D], gT[:, k, lo_c:lo_c + n_c],
                                       start=(k == 0), stop=(k == KH - 1))
                elif name == "next":
                    done(pe, it, off, ("down", 0), ("down", 1), bank=bank)
                    for t in ((0, 1, 2, 3), (4,))[part]:
                        mm = pe.matmul(o[0:rows(t), (t % 4) * P:(t % 4 + 1) * P], yT[:, t * P:t * P + rows(t)], wn, start=True, stop=True)
                mm.then_inc(spare_full[bank], 1)

            def body(it):
                for phase in (X, Y):
                    for slot in range(TILES):
                        for work in plan.ORDER["pe", phase]:
                            tile = plan.tile(it, phase, slot, LAG if work == "turn" else 0)
                            if work == "units":
                                now = slot - LEAD
                                for n, u in enumerate(plan.slot_units(it, phase, now)):
                                    unit(it, phase, now, n, u)
                                for step in range(1, len(plan.BLOCKS)):
                                    for n, u in enumerate(plan.slot_units(it, phase, now - step)):
                                        if u[0][:2] == "pv":
                                            values(it, phase, now - step, n, u, plan.BLOCKS[step])
                            elif tile:
                                (score if work == "score" else turn)(it, tile)

            iterations(pe, body)

        @block.scalar
        def _(act):
            def exponent(it, tile):
                phase, off, k, back = tile
                m = rows(k // H)
                n = plan.number(it, tile)
                if phase == 0:
                    act.wait_ge(top_found, batch(it, off, TILES, k + 1))
                    act.activation(nbias[0:m, k % 2:k % 2 + 1], top[0:m, k % 2, 0:1], ACT.Copy, scale=-1.0).then_inc(bias_ready[0], 1)
                act.wait_ge(bias_ready[phase], batch(it, off, TILES, k + 1))
                src = scores[0:m, k % 2, S0:S0 + C]
                bias = nbias[0:m, k % 2:k % 2 + 1]
                if phase == 0:
                    act.activation(expd[0:m, k % 2, :], src, ACT.Exp, bias=bias).then_inc(exp_done, 1)
                else:
                    if it.looped or n >= PROBS:
                        act.wait_ge(turned_full, 2 * n - 2 * PROBS + 2)
                    act.activation(prob[0:m, k % PROBS, 0:C], src, ACT.Exp, bias=bias,
                                   accum_out=rsum[0:m, k:k + 1]).then_inc(probs_ready[k % 2], 1)

            def unit(it, phase, slot, n, u):
                name, off, part = u
                if plan.TAKER.get(name) != "act":
                    return
                bank, used, _ = plan.bank(it, phase, slot, n)
                act.wait_ge(spare_full[bank], used + 1)
                take(act, act.copy, lambda o, i, b: act.activation(o, i, ACT.Identity, bias=b), it, name, off, part, bank)

            def copy_out(it, tile):
                for part in (0, 1):
                    if plan.COPIES[tile[0]][tile[2] % 4][part] == "act":
                        copy_block(act, act.copy, it, tile, part)

            def job(it, phase, slot, name, off, part):
                if name == "gelu_out":
                    done(act, it, off, ("next", 0), ("next", 1))
                    if it.looped or it.like + off >= 1:
                        act.wait_ge(stored, batch(it, off, 32, 0))
                    act.activation(gz[:], z[:], ACT.Gelu).then_inc(gz_ready, 1)
                elif name == "gelu_up":
                    done(act, it, off, ("up", 2 * KH - 2), ("up", 2 * KH - 1))
                    act.activation(gT[:], gT[:], ACT.Gelu).then_inc(hidden_ready, 1)

            def body(it):
                for phase in (X, Y):
                    for slot in range(TILES):
                        tile = plan.tile(it, phase, slot)
                        if tile:
                            exponent(it, tile)
                        for work in plan.ORDER["act", phase]:
                            if work == "results":
                                for place, n, u in plan.results(it, phase, slot, "act"):
                                    unit(it, phase, place, n, u)
                            elif work == "copies":
                                tile = plan.tile(it, phase, slot, LAG)
                                if tile:
                                    copy_out(it, tile)
                            else:
                                for name, off, part in plan.JOBS[phase].get(slot, []):
                                    if plan.has(it, off):
                                        job(it, phase, slot, name, off, part)

            act.wait_ge(prep_v, 14)
            iterations(act, body)

        @block.vector
        def _(dve):
            for n, buf in enumerate((val[0], val[1], hraw, hh, z)):
                dve.memset(buf[:, NT - 1, :], 0.0).then_inc(prep_v, 1)
            dve.wait_ge(consts_in, 48)
            dve.wait_ge(prep_p, 1)
            dve.tensor_tensor(bo1, spare[:, 1, 1:2], bo1, ALU.add).then_inc(prep_v, 1)
            dve.tensor_scalar(wf[:, 0, :], spare[:, 0, 0:P], SCALE, None, ALU.mult).then_inc(prep_v, 1)
            dve.tensor_copy(wf[:, 1:3, :], spare[:, 0, P:3 * P].rearrange("p (n f) -> p n f", n=2)).then_inc(prep_v, 1)
            dve.tensor_scalar(wg[:], wa, ln_g, None, ALU.mult).then_inc(prep_v, 1)
            dve.tensor_scalar(wq1, wq1, SCALE, None, ALU.mult).then_inc(prep_v, 1)
            dve.tensor_scalar(fcol[:, 0:1], bq1, SCALE, None, ALU.mult).then_inc(prep_v, 1)
            dve.wait_ge(prep_p, 2)
            dve.tensor_tensor(fcol[:, 3:4], spare[:, 1, 0:1], battn, ALU.add)
            dve.tensor_scalar(fcol[:, 1:2], spare[:, 1, 2:3], bq2, SCALE, ALU.add, ALU.mult)
            dve.tensor_tensor(fcol[:, 2:3], spare[:, 1, 3:4], bk2, ALU.add)
            dve.tensor_tensor(bv2, spare[:, 1, 4:5], bv2, ALU.add).then_inc(prep_v, 1)
            dve.wait_ge(prep_v, 12)
            dve.tensor_copy(bv2_wide[:], bv2.broadcast_to((P, P))).then_inc(prep_v, 1)
            dve.wait_ge(prep_p, 3)
            dve.tensor_tensor(bo2_row, spare[:, 1, P:2 * P], bo2_row, ALU.add).then_inc(prep_v, 1)
            dve.wait_ge(prep_v, 14)

            def maximum(it, tile):
                phase, off, k, back = tile
                m = rows(k // H)
                n = plan.number(it, tile)
                src = scores[0:m, k % 2, S0:S0 + C]
                if phase == 0:
                    alone(dve, scores_full, n + 1)
                    dve.max(top[0:m, k % 2, :], src).then_inc(top_found, 1)
                else:
                    dve.wait_ge(scores_full, n + 1)
                    dve.tensor_reduce(nbias[0:m, k % 2:k % 2 + 1], src, AX.X, ALU.max, negate=True).then_inc(bias_ready[1], 1)

            def mask(it, tile):
                phase, off, k, back = tile
                if phase == 1:
                    return
                m = rows(k // H)
                n = plan.number(it, tile)
                if it.looped or n >= PROBS:
                    dve.wait_ge(turned_full, 2 * n - 2 * PROBS + 2)
                dve.wait_ge(exp_done, batch(it, off, TILES, k + 1))
                dve.scalar_tensor_tensor(prob[0:m, k % PROBS, 0:C], scores[0:m, k % 2, S0:S0 + C], top[0:m, k % 2, TOPK - 1:TOPK],
                                         expd[0:m, k % 2, :], ALU.is_ge, ALU.mult,
                                         accum_out=rsum[0:m, k:k + 1]).then_inc(probs_ready[k % 2], 1)

            def copy_out(it, tile):
                for part in (0, 1):
                    if plan.COPIES[tile[0]][tile[2] % 4][part] == "dve":
                        copy_block(dve, dve.tensor_copy, it, tile, part)

            def job(it, phase, slot, name, off, part):
                if name in ("inverse1", "inverse2"):
                    a = 0 if name == "inverse1" else 1
                    tiles = HALF_TILES[part]
                    k0, k1 = tiles[0] * H, (tiles[-1] + 1) * H
                    for par in (0, 1):
                        dve.wait_ge(probs_ready[par], attention_count(it, phase, part, TILES // 2, k1 // 2))
                    groups = ((0, 3),) if part == 0 else ((3, 4), (4, 5))
                    for t0, t1 in groups:
                        m = rows(t0)
                        dve.reciprocal(rinv[0:m, t0 * H:t1 * H], rsum[0:m, t0 * H:t1 * H]).then_inc(inverse_found, 1)
                    before = half_before(it, off, a, part)
                    if before:
                        computed(dve, it, before[1], before[0][0].replace("pv", "spread"), before[0][1])
                    dve.wait_ge(inverse_found, attention_count(it, phase, part, 3, (1, 3)[part]))
                    for t0, t1 in groups:
                        m, at = rows(t0), (t0 - tiles[0]) * H
                        dve.tensor_copy(rwide[0:m, at:at + (t1 - t0) * H, :],
                                        rinv[0:m, t0 * H:t1 * H].unsqueeze(2).broadcast_to((m, (t1 - t0) * H, DK))).then_inc(wide_ready, 1)
                elif name in ("stats_h", "stats_hh", "stats_h2"):
                    s, buf = {"stats_h": (0, hraw), "stats_hh": (1, hh), "stats_h2": (2, h2)}[name]
                    if s == 0:
                        done(dve, it, off, ("mdct", 0), ("mdct", 1))
                    elif s == 1:
                        done(dve, it, off, ("wo2", 0), ("wo2", 1))
                    else:
                        dve.wait_ge(h2_ready, batch(it, off, 1, 1))
                    for t in range(NT):
                        dve.bn_stats(stat[:, s, t, :], buf[:, t, :]).then_inc(stats_part[s], 1)
                    alone(dve, stats_part[s], batch(it, off, NT, NT))
                    for t in range(NT):
                        dve.bn_aggr(mv[:, s, t, :], stat[:, s, t, :]).then_inc(stats_ready[s], 1)

            def unit(it, phase, slot, n, u):
                name, off, part = u
                if plan.TAKER.get(name, "dve") != "dve":
                    return
                bank, used, _ = plan.bank(it, phase, slot, n)
                a = 0 if name.endswith("1") else 1
                o = spare[:, bank, :]
                tiles = ((0, 4), (4, 5))[part % 2]
                m = rows(tiles[0])
                nt = tiles[1] - tiles[0]
                natural = o[0:m, 0:nt * P].rearrange("p (t f) -> p t f", t=nt)
                dve.wait_ge(spare_full[bank], used + 1)
                if name in plan.TAKER:
                    take(dve, dve.tensor_copy, lambda o, i, b: dve.tensor_scalar(o, i, b, None, ALU.add), it, name, off, part, bank)
                    return
                if name in ("pv1", "pv2"):
                    lo_c, n_c = HALF[part]
                    done(dve, it, off, ("spread" + name[-1], part))
                    dve.tensor_tensor(attnT[a][:, lo_c:lo_c + n_c], o[:, 0:n_c], spread[:, 0:n_c], ALU.mult).then_inc(spare_free[bank], 1)
                    return
                elif name == "wo2":
                    if part == 0:
                        dve.wait_ge(spill_in, batch(it, off, 16, 16))
                    xb = hxp[:, 1, :].rearrange("p (t f) -> p t f", t=NT)
                    i = dve.tensor_tensor(hh[0:m, tiles[0]:tiles[1], :], natural, xb[0:m, tiles[0]:tiles[1], :], ALU.add)
                elif name == "next":
                    if part == 0 and (it.looped or it.like + off >= 1):
                        dve.wait_ge(gz_ready, batch(it, off, 1, 0))
                    i = dve.tensor_tensor(z[0:m, tiles[0]:tiles[1], :], natural,
                                          next_row[0:m].unsqueeze(1).broadcast_to((m, nt, D)), ALU.add)
                i.then_inc(spare_free[bank], 1)

            def body(it):
                for phase in (X, Y):
                    for slot in range(TILES):
                        tile = plan.tile(it, phase, slot)
                        if tile:
                            maximum(it, tile)
                        for lag in ((1, 0) if slot % 2 else ()):
                            tile = plan.tile(it, phase, slot, lag)
                            if tile:
                                mask(it, tile)
                        for work in plan.ORDER["dve", phase]:
                            if work == "results":
                                for place, n, u in plan.results(it, phase, slot, "dve"):
                                    unit(it, phase, place, n, u)
                            elif work == "copies":
                                tile = plan.tile(it, phase, slot, LAG)
                                if tile:
                                    copy_out(it, tile)
                            else:
                                for name, off, part in plan.JOBS[phase].get(slot, []):
                                    if plan.has(it, off):
                                        job(it, phase, slot, name, off, part)

            iterations(dve, body)

        @block.gpsimd
        def _(pool):
            pool.memset(ident[:], 0.0).then_inc(prep_g, 1)
            pool.memset(half_neg[:], -0.5).then_inc(prep_g, 1)
            pool.memset(prob[:, :, C:CP], 0.0).then_inc(prep_g, 1)
            pool.wait_ge(prep_g, 3)
            pool.affine_select(out=ident[:], in_=ident[:], compare_op=ALU.not_equal, fill=1.0, base=0,
                               pattern=[[-1, P]], channel_multiplier=1).then_inc(prep_g, 1)

            def norm(it, off, s, step, k):
                def before(n):
                    alone(pool, step, batch(it, off, STEPS[s], k + n))
                alone(pool, stats_ready[s], batch(it, off, NT, NT))
                pool.tensor_scalar(ve[:, s, :], mv[:, s, :, 1], EPS, 1.0, ALU.add, ALU.mult).then_inc(step, 1)
                before(1)
                pool.tensor_tensor(rstd[:, s, :], ve[:, s, :], half_neg[:], ALU.pow).then_inc(step, 1)
                before(2)
                pool.tensor_tensor(negm[:, s, :], mv[:, s, :, 0], rstd[:, s, :], ALU.mult).then_inc(step, 1)
                before(3)
                pool.tensor_scalar(shift[:, s, :], negm[:, s, :], -1.0, 1.0, ALU.mult, ALU.mult).then_inc(step, 1)
                before(4)

            def scaled(dst, src, scale, add, ready):
                for t in range(NT):
                    pool.tensor_scalar(dst[:, t, :], src[:, t, :], scale[:, t:t + 1],
                                       add if isinstance(add, float) else add[:, t:t + 1], ALU.mult, ALU.add).then_inc(ready, 1)

            def wide(r):
                return r.unsqueeze(1).broadcast_to((P, NT, D))

            hx_t = hx[:].rearrange("p a (t f) -> p a t f", t=NT)
            hxp_t = hxp[:].rearrange("p a (t f) -> p a t f", t=NT)

            def front(it, off):
                norm(it, off, 0, norm_step[0], 0)
                if it.looped or it.like + off >= 1:
                    computed(pool, it, off - 1, "turn", 1)
                    pool.sem_inc(passed, 1)
                scaled(x1, hraw, rstd[:, 0, :], shift[:, 0, :], x1_ready)
                if it.looped or it.like + off >= 1:
                    alone(pool, spill_out, batch(it, off, 16, 0))
                pool.tensor_tensor(hx_t[:, 0], hraw[:], wide(beta_row), ALU.add).then_inc(hx_ready, 1)
                pool.wait_ge(x1_ready, batch(it, off, NT, NT))
                pool.tensor_tensor(hx_t[:, 1], x1[:], wide(bo2_row), ALU.add).then_inc(hx_ready, 1)

            def post(it, off):
                norm(it, off, 1, norm_step[1], 0)
                if it.looped or it.like + off >= 1:
                    computed(pool, it, off - 1, "mix", 1)
                    pool.sem_inc(passed, 1)
                scaled(xf, hh, rstd[:, 1, :], shift[:, 1, :], norm_step[1])
                pool.wait_ge(norm_step[1], batch(it, off, STEPS[1], 4 + NT))
                pool.tensor_tensor(xf[:], xf[:], wide(gamma_row), ALU.mult).then_inc(norm_step[1], 1)
                if it.looped or it.like + off >= 1:
                    pool.wait_ge(h2_kept, batch(it, off, 16, 0))
                pool.wait_ge(norm_step[1], batch(it, off, STEPS[1], 5 + NT))
                pool.tensor_tensor(h2[:], xf[:], hxp_t[:, 0], ALU.add).then_inc(h2_ready, 1)

                step = norm_step[2]
                norm(it, off, 2, step, 0)
                pool.tensor_tensor(var_x[:, 0, :], mv[:, 2, :, 1], rstd[:, 2, :], ALU.mult).then_inc(step, 1)
                pool.wait_ge(step, batch(it, off, STEPS[2], 5))
                pool.tensor_tensor(var_x[:, 1, :], var_x[:, 0, :], rstd[:, 2, :], ALU.mult).then_inc(step, 1)
                alone(pool, step, batch(it, off, STEPS[2], 6))
                pool.tensor_scalar(var_x[:, 0, :], var_x[:, 1, :], EPS, 1.0, ALU.add, ALU.mult).then_inc(step, 1)
                pool.wait_ge(step, batch(it, off, STEPS[2], 7))
                pool.tensor_tensor(rstd_x[:], var_x[:, 0, :], half_neg[:], ALU.pow).then_inc(step, 1)
                scaled(xf, h2, rstd[:, 2, :], shift[:, 2, :], step)
                if it.looped or it.like + off >= 1:
                    computed(pool, it, off - 1, "turn_n", 1)
                    pool.sem_inc(passed, 1)
                alone(pool, step, batch(it, off, STEPS[2], 8 + NT))
                scaled(nrm, xf, rstd_x, 0.0, nrm_ready)

            def split_operands(it, off, a):
                for w in (0, 1):
                    for part in (0, 1):
                        done(pool, it, off, ("qk"[w] + "12"[a], part))
                        pool.sem_inc(passed, 1)
                    pool.tensor_scalar(hi[:, w, :], lo[:, w, :].bitcast(F32), 1.0, 0.0, ALU.mult, ALU.add).then_inc(split[a], 1)
                for w in (0, 1):
                    pool.wait_ge(split[a], batch(it, off, 4, 1 + w))
                    whole = lo[:, w, :].bitcast(F32)
                    pool.tensor_tensor(lo[:, w, :], whole, hi[:, w, :].bitcast(F32), ALU.subtract).then_inc(split[a], 1)

            def final(it, off):
                pool.wait_ge(gz_ready, batch(it, off, 1, 1))
                pool.wait_ge(h2_kept, batch(it, off, 16, 16))
                pool.tensor_tensor(gz[:], gz[:], h2_old[:], ALU.add).then_inc(out_ready, 1)

            def body(it):
                if plan.has(it, 1):
                    front(it, 1)
                if plan.has(it, -1):
                    split_operands(it, -1, 1)
                if plan.has(it, -2):
                    post(it, -2)
                if plan.has(it, 1):
                    split_operands(it, 1, 0)
                if plan.has(it, -3):
                    final(it, -3)

            pool.wait_ge(consts_in, 48)
            pool.wait_ge(prep_v, 14)
            iterations(pool, body)


def kernel(**inputs):
    import concourse.bacc as bacc
    from concourse.bass_utils import run_bass_kernel_spmd

    arr = {k: np.ascontiguousarray(v) for k, v in inputs.items()}
    attn = {k[len("L0_attn_"):]: v for k, v in arr.items() if k.startswith("L0_attn_")}
    ffn = {k[len("L0_ffn_"):]: v for k, v in arr.items() if k.startswith("L0_ffn_")}
    x = arr["x"]
    batches, samples = x.shape

    blocks = np.zeros((batches, C + 1, P), np.float32)
    blocks.reshape(batches, -1)[:, P:P + samples] = x
    xT = np.ascontiguousarray(blocks.transpose(0, 2, 1))

    length = 2 * P
    n = np.arange(length, dtype=np.float32) + np.float32(0.5)
    k = np.float32(np.pi / P) * n[:P]
    table = np.sqrt(np.float32(4.0 / P)) * np.cos((n + np.float32(P / 2))[:, None] * k[None, :])
    window = np.sin(np.float32(np.pi) * n / np.float32(length))
    mdct = (window[:, None] * table).astype(np.float32)

    mats = np.ascontiguousarray(np.stack(
        [attn["Wq1"].T, attn["Wk1"].T, attn["Wv1"].T, attn["Wo1"], attn["Wq2"].T, attn["Wk2"].T, attn["Wv2"].T,
         attn["Wo2"].T, ffn["attn_w"].T, ffn["next_w"].T, mdct[:P], mdct[P:], attn["Wo1"].T], axis=1))
    cols = np.ascontiguousarray(np.stack(
        [attn["bq1"], attn["bk1"], attn["bo1"], attn["bq2"], attn["bk2"], ffn["ln_g"], ffn["ln_b"], ffn["attn_b"],
         attn["bv1"], attn["bv2"]], axis=1))
    rows_in = np.stack([attn["bo2"], attn["gamma"], attn["beta"], ffn["next_b"]])
    e = ffn["fc1_w"].shape[0]
    experts = np.concatenate(
        [ffn["fc1_w"].transpose(0, 2, 1),
         ffn["fc2_w"].transpose(0, 2, 1).reshape(e, KH, P, D).transpose(0, 2, 1, 3).reshape(e, P, KH * D),
         ffn["fc1_b"].reshape(e, KH, P).transpose(0, 2, 1), ffn["fc2_b"][:, :, None]], axis=2)
    experts = np.ascontiguousarray(np.concatenate([experts, experts]))

    given = {"xT": xT, "mats": mats, "cols": cols, "rows_in": rows_in, "experts": experts}
    nc = bacc.Bacc("TRN2", target_bir_lowering=False, num_devices=1)
    aps = {name: nc.dram_tensor(name, a.shape, F32, kind="ExternalInput").ap() for name, a in given.items()}
    out = nc.dram_tensor("out", (batches, C, D), F32, kind="ExternalOutput").ap()
    build(nc, **aps, out=out)
    result = run_bass_kernel_spmd(nc, [given], core_ids=[0])
    return result.results[0]["out"]
```

```python
from contextlib import ExitStack

import numpy as np

import concourse.bass as bass
from concourse import mybir

F32 = mybir.dt.float32
F32R = mybir.dt.float32r
ALU = mybir.AluOpType
ACT = mybir.ActivationFunctionType
AX = mybir.AxisListType

P = 128
C = 626
D = 128
H = 4
DK = D // H
TOPK = 5
NT = -(-C // P)
CP = NT * P
HID = 512
KH = HID // P
EPS = 1e-5
SCALE = float(DK) ** -0.5
TILES = NT * H
HALF = ((0, 384), (384, C - 384))
HALF_TILES = ((0, 1, 2), (3, 4))
S0, S1 = 198, 512
N0 = S1 - S0
NORM = 11
STEPS = (NORM, NORM + 1 + NT, NORM + 4 + NT)
PROBS = 4
LAG = 3
LEAD = 1


def rows(t):
    return min(P, C - t * P)


class Iteration:

    def __init__(self, index, first=None):
        self.index, self.looped = index, first is not None
        self.like = first if self.looped else index

    def at(self, f):
        if not self.looped:
            return f(self.index)
        start, step = f(self.like), f(self.like + 1) - f(self.like)
        return self.index * step + (start - step * self.like)


class Plan:

    X, Y = 0, 1

    UNITS = {
        X: {
            0: [("mdct", 1, 0), ("mdct", 1, 1)],
            1: [("v1", 0, 0), ("v1", 0, 1)],
            2: [("k2", -1, 0), ("k2", -1, 1)],
            3: [("spread2", -2, 1), ("pv2", -2, 1)],
            8: [("wo2", -2, 0), ("wo2", -2, 1)],
            9: [("down", -3, 0)],
            10: [("down", -3, 1)],
            11: [("v2", -1, 0), ("v2", -1, 1)],
            12: [("turn", 1, 0), ("turn", 1, 1)],
            13: [("q1", 1, 0), ("q1", 1, 1)],
            14: [("spread1", 0, 0), ("pv1", 0, 0)],
        },
        Y: {
            0: [("k1", 1, 0)],
            1: [("k1", 1, 1), ("turn_n", -2, 0)],
            2: [("turn_n", -2, 1)],
            3: [("spread1", 0, 1), ("pv1", 0, 1)],
            8: [("mix", -2, 0), ("mix", -2, 1)],
            9: [("up", -2, 0), ("next", -3, 0), ("next", -3, 1)],
            10: [("up", -2, 1), ("up", -2, 2)],
            11: [("q2", 0, 0), ("q2", 0, 1)],
            12: [("up", -2, 3), ("up", -2, 4), ("up", -2, 5)],
            13: [("up", -2, 6), ("up", -2, 7)],
            14: [("spread2", -1, 0), ("pv2", -1, 0)],
        },
    }
    BLOCKS = ((0,), (1,), (2,), (3,), (4,))
    TAKER = {"q1": ("act", "act"), "k1": ("act", "act"), "q2": ("act", "act"), "k2": ("act", "act"),
             "v1": ("act", "act"), "v2": ("act", "act"), "mdct": ("act", "act"), "turn": ("dve", "act"),
             "turn_n": ("act", "dve"), "spread1": ("dve", "dve"), "spread2": ("act", "act"), "mix": ("dve", "act"),
             "up": ("dve", "dve", "dve", "dve", "dve", "dve", "dve", "act"), "down": ("act", "act"),
             "wo2": ("dve", "dve"), "next": ("act", "act")}
    COPIES = {X: [("act", "act"), ("dve", "act"), ("act", "act"), ("dve", "act")],
              Y: [("dve", "dve"), ("dve", "dve"), ("dve", "dve"), ("dve", "act")]}
    LATE = {"act": {"spread2": 2, "q2": 0}, "dve": {}}
    ORDER = {("pe", X): ("score", "turn", "units"),
             ("pe", Y): ("score", "turn", "units"),
             ("act", X): ("copies", "results", "jobs"),
             ("act", Y): ("copies", "results", "jobs"),
             ("dve", X): ("results", "copies", "jobs", "mask"),
             ("dve", Y): ("copies", "jobs", "results")}
    JOBS = {
        X: {
            2: [("inverse2", -2, 1)],
            3: [("stats_h", 1, 0)],
            10: [("stats_hh", -2, 0)],
            12: [("inverse1", 0, 0)],
            16: [("stats_h2", -2, 0)]},
        Y: {
            2: [("inverse1", 0, 1)],
            13: [("gelu_out", -3, 0)],
            14: [("inverse2", -1, 0)],
            15: [("gelu_up", -2, 0)]},
    }

    def __init__(self, batches):
        self.batches = batches
        self.loop = (4, batches - 2)
        self.unit_total = {}

    def has(self, it, offset):
        return it.looped or 0 <= it.like + offset < self.batches

    def phase_exists(self, j, phase):
        return 0 <= j - phase < self.batches

    def phases_before(self, j, phase=0):
        n = sum(self.phase_exists(i, q) for i in range(j) for q in (0, 1))
        return n + (phase == 1 and self.phase_exists(j, 0))

    def tile(self, it, phase, slot, lag=0):
        k, back = slot - lag, 0
        if k < 0:
            k += TILES
            phase, back = (0, 0) if phase == 1 else (1, 1)
        if not it.looped and not self.phase_exists(it.like - back, phase):
            return None
        return phase, -back - phase, k, back

    def number(self, it, tile):
        phase, _, k, back = tile
        return it.at(lambda j: TILES * self.phases_before(j - back, phase) + k)

    def slot_units(self, it, phase, slot):
        return [u for u in self.UNITS[phase].get(slot, []) if self.has(it, u[1])]

    def taker(self, name, part):
        takers = self.TAKER.get(name, ("dve",))
        return takers[part % len(takers)]

    def results(self, it, phase, slot, engine):
        found = []
        for place in range(slot - len(self.BLOCKS) - 1, slot + 1):
            for n, u in enumerate(self.slot_units(it, phase, place)):
                last = len(self.BLOCKS) - 1 if u[0][:2] == "pv" else 0
                if place + last + self.LATE[engine].get(u[0], LEAD) == slot:
                    found.append((place, n, u))
        return found

    def units_before(self, j, phase, slot, n):
        if j not in self.unit_total:
            self.unit_total[j] = sum(self.units_in(i, 2, 0) for i in range(-1, j))
        return self.unit_total[j] + self.units_in(j, phase, slot) + n

    def units_in(self, j, phase, slot):
        return sum(
            0 <= j + u[1] < self.batches
            for q in (0, 1) for s, us in self.UNITS[q].items() if (q, s) < (phase, slot) for u in us
        )

    def bank(self, it, phase, slot, n):
        u = self.units_before(it.like, phase, slot, n)
        return u % 2, it.at(lambda j: self.units_before(j, phase, slot, n) // 2), u < 2

    def place(self, name, part):
        for phase, slots in self.UNITS.items():
            for slot, units in slots.items():
                for n, u in enumerate(units):
                    if (u[0], u[2]) == (name, part):
                        return phase, slot, n, u[1]
        raise KeyError(name)

    def unit_count(self, it, offset, name, part):
        phase, slot, n, own = self.place(name, part)
        back = own - offset

        def number(j):
            present = self.UNITS[phase][slot][:n]
            before = sum(0 <= j + u[1] < self.batches for u in present)
            return self.units_before(j, phase, slot, before)

        u = number(it.like - back)
        return u % 2, it.at(lambda j: number(j - back) // 2 + 1)


def build(nc, xT, mats, cols, rows_in, experts, out):
    B = xT.shape[0]
    plan = Plan(B)
    X, Y = Plan.X, Plan.Y
    NM, NCOL, NROW = mats.shape[1], cols.shape[1], rows_in.shape[0]
    spill = nc.dram_tensor("spill", [B, P, 2 * CP], F32).ap()

    with ExitStack() as ctx:
        def sb(name, shape, dt=F32):
            return ctx.enter_context(nc.sbuf_tensor(name, shape, dt))

        def sem(name):
            return ctx.enter_context(nc.semaphore(name))

        scores = ctx.enter_context(nc.psum_tensor("scores", [P, 2, 1024], F32))
        turned = ctx.enter_context(nc.psum_tensor("turned", [P, 2, 512], F32))
        spare = ctx.enter_context(nc.psum_tensor("spare", [P, 2, 512], F32))

        mat = sb("mat", [P, NM, P])
        col = sb("col", [P, NCOL])
        row = sb("row", [P, NROW, D])
        ident = sb("ident", [P, P])
        wq1, wk1, wv1, wo1, wq2, wk2, wv2, wo2, wa, wn = (mat[:, i, :] for i in range(10))
        wo1_turned = mat[:, 12, :]
        mdct = [mat[:, 10, :], mat[:, 11, :]]
        bq1, bk1, bo1, bq2, bk2, ln_g, ln_b, battn, bv1, bv2 = (col[:, i:i + 1] for i in range(10))
        bo2_row, gamma_row, beta_row, next_row = (row[:, i, :] for i in range(4))
        wf = sb("wf", [P, 3, P])
        wg = sb("wg", [P, P])
        fcol = sb("fcol", [P, 5])
        bv2_wide = sb("bv2_wide", [P, P])
        half_neg = sb("half_neg", [P, NT])

        xt = sb("xt", [P, C + 1])
        hx = sb("hx", [P, 2, CP])
        hxp = sb("hxp", [P, 2, CP])
        hraw = sb("hraw", [P, NT, D])
        x1 = sb("x1", [P, NT, D])
        x1T = sb("x1T", [P, CP])
        hi = [sb(f"hi{a}", [P, 2, C], F32R) for a in (1, 2)]
        lo = [sb(f"lo{a}", [P, 2, C], F32R) for a in (1, 2)]
        stack = [sb(f"stack{a}", [3 * DK, 2, H, C], F32R) for a in (1, 2)]
        val = [sb(f"val{a}", [P, NT, D]) for a in (1, 2)]
        top = sb("top", [P, 2, 8])
        nbias = sb("nbias", [P, 2])
        expd = sb("expd", [P, 2, C])
        prob = sb("prob", [P, PROBS, CP])
        rsum = sb("rsum", [P, TILES])
        rinv = sb("rinv", [P, TILES])
        rwide = sb("rwide", [P, 3 * H, DK])
        probT = [sb(f"probT{n}", [P, H, NT, HALF[n][1]]) for n in (0, 1)]
        spread = sb("spread", [P, HALF[0][1]])
        attnT = [sb(f"attnT{a}", [P, C]) for a in (1, 2)]
        hh = sb("hh", [P, NT, D])
        h2 = sb("h2", [P, NT, D])
        h2_old = sb("h2_old", [P, NT, D])
        xf = sb("xf", [P, NT, D])
        nrm = sb("nrm", [P, NT, D])
        nrmT = sb("nrmT", [P, CP])
        xaT = sb("xaT", [P, C])
        expert = sb("expert", [P, experts.shape[2]])
        gT = sb("gT", [P, KH, C])
        yT = sb("yT", [P, C])
        z = sb("z", [P, NT, D])
        gz = sb("gz", [P, NT, D])
        stat = sb("stat", [P, 3, NT, 6])
        part = sb("part", [P, 3, 5, NT])
        var = sb("var", [P, 3, NT])
        ve = sb("ve", [P, 3, NT])
        rstd = sb("rstd", [P, 3, NT])
        negm = sb("negm", [P, 3, NT])
        shift = sb("shift", [P, 3, NT])
        var_x = sb("var_x", [P, 2, NT])
        rstd_x = sb("rstd_x", [P, NT])

        consts_in = sem("consts_in")
        prep_v, prep_p, prep_g = sem("prep_v"), sem("prep_p"), sem("prep_g")
        x_in = sem("x_in")
        spill_out, spill_in = sem("spill_out"), sem("spill_in")
        stacked = [sem("stacked1"), sem("stacked2")]
        expert_in = sem("expert_in")
        h2_kept = sem("h2_kept")
        stored = sem("stored")
        spare_full = [sem("spare_full0"), sem("spare_full1")]
        spare_free = [sem("spare_free0"), sem("spare_free1")]
        scores_full = sem("scores_full")
        top_found = sem("top_found")
        bias_ready = [sem("bias_ready1"), sem("bias_ready2")]
        exp_done = sem("exp_done")
        probs_ready = [sem("probs_ready0"), sem("probs_ready1")]
        turned_full = sem("turned_full")
        turned_free = [sem("turned_free0"), sem("turned_free1")]
        inverse_found = sem("inverse_found")
        wide_ready = sem("wide_ready")
        stats_part = [sem(f"stats_part{n}") for n in range(3)]
        passed = sem("passed")
        norm_step = [sem(f"norm_step{n}") for n in range(3)]
        x1_ready = sem("x1_ready")
        hx_ready = sem("hx_ready")
        split = [sem("split1"), sem("split2")]
        hh_ready = sem("hh_ready")
        z_biased = sem("z_biased")
        h2_ready = sem("h2_ready")
        nrm_ready = sem("nrm_ready")
        hidden_ready = sem("hidden_ready")
        gz_ready = sem("gz_ready")
        out_ready = sem("out_ready")

        def batch(it, offset, per, k):
            return it.at(lambda j: (j + offset) * per + k)

        def alone(engine, s, value):
            engine.wait_ge(s, value)
            engine.sem_inc(passed, 1)

        def done(engine, it, offset, *units, bank=None):
            counts = dict(plan.unit_count(it, offset, *unit) for unit in units)
            for b, count in counts.items():
                if b != bank:
                    engine.wait_ge(spare_free[b], count)

        def computed(engine, it, offset, name, part):
            bank, count = plan.unit_count(it, offset, name, part)
            engine.wait_ge(spare_full[bank], count)

        def attention(phase, part):
            return (phase, 0) if part == 0 else ((0, 0) if phase == 1 else (1, 1))

        def attention_count(it, phase, part, per, k):
            phase, back = attention(phase, part)
            return it.at(lambda j: per * plan.phases_before(j - back, phase) + k)

        def half_before(it, off, a, part):
            found = {(0, 0): [(("pv2", 1), -2), (("pv1", 1), -1)], (0, 1): [(("pv1", 0), 0)],
                     (1, 0): [(("pv1", 1), 1), (("pv2", 1), -1)], (1, 1): [(("pv2", 0), 0)]}[a, part]
            return next(((u, off + d) for u, d in found if plan.has(it, off + d)), None)

        def product_before(it, off, a, half):
            found = (("pv2", -2), ("pv1", -1)) if a == 0 else (("pv1", 1), ("pv2", -1))
            return next(((u, off + d) for u, d in found if plan.has(it, off + d)), None)

        def copy_block(engine, copy, it, tile, part):
            phase, off, k, back = tile
            t, h = divmod(k, H)
            m = rows(t)
            n = plan.number(it, tile)
            half = 0 if t in HALF_TILES[0] else 1
            at = t * P - HALF[half][0]
            if t == HALF_TILES[half][0] and h == 0:
                before = product_before(it, off, phase, half)
                if before:
                    computed(engine, it, before[1], before[0], half)
            engine.wait_ge(turned_full, 2 * n + part + 1)
            blocks = ((0, 3), (3, 5))[part]
            src = turned[:, part, 0:(blocks[1] - blocks[0]) * P].rearrange("p (j c) -> p j c", c=P)[:, :, 0:m]
            copy(probT[half][:, h, blocks[0]:blocks[1], at:at + m], src).then_inc(turned_free[part], 1)

        def take(engine, copy, biased, it, name, off, part, bank):
            o = spare[:, bank, :]
            if name in ("mdct", "turn", "turn_n"):
                lo_c, n_c = ((0, 4 * P), (4 * P, P))[part]
            elif name != "up":
                lo_c, n_c = HALF[part]
            if name == "mdct":
                if part == 0:
                    if it.looped or it.like + off >= 1:
                        engine.wait_ge(hx_ready, batch(it, off, 2, 0))
                    i = copy(hraw[:, 0:4, :], o.rearrange("p (t f) -> p t f", t=4))
                else:
                    i = copy(hraw[0:rows(4), 4, :], o[0:rows(4), 0:P])
            elif name in ("turn", "turn_n"):
                i = copy((x1T if name == "turn" else nrmT)[:, lo_c:lo_c + n_c], o[:, 0:n_c])
            elif name in ("spread1", "spread2"):
                before = half_before(it, off, int(name[-1]) - 1, part)
                if before:
                    done(engine, it, before[1], before[0])
                i = copy(spread[:, 0:n_c], o[:, 0:n_c])
            elif name[0] in "qk":
                a, w = int(name[-1]) - 1, int(name[0] == "k")
                if (w, part) == (0, 0) and (it.looped or it.like + off >= 1):
                    engine.wait_ge(stacked[a], batch(it, off, 384, 0))
                bias = ((fcol[:, 0:1], bk1), (fcol[:, 1:2], fcol[:, 2:3]))[a][w]
                i = biased(lo[a][:, w, lo_c:lo_c + n_c].bitcast(F32), o[:, 0:n_c], bias)
            elif name[0] == "v":
                tiles = ((0, 4), (4, 5))[part]
                m, nt = rows(tiles[0]), tiles[1] - tiles[0]
                i = copy(val[int(name[-1]) - 1][0:m, tiles[0]:tiles[1], :], o[0:m, 0:nt * P].rearrange("p (t f) -> p t f", t=nt))
            elif name in ("wo2", "next"):
                if part == 0 and (it.looped or it.like + off >= 1):
                    if name == "wo2":
                        computed(engine, it, off - 1, "mix", 1)
                    else:
                        engine.wait_ge(z_biased, batch(it, off, 1, 0))
                tiles = ((0, 4), (4, 5))[part]
                m, nt = rows(tiles[0]), tiles[1] - tiles[0]
                i = copy((xf if name == "wo2" else z)[0:m, tiles[0]:tiles[1], :], o[0:m, 0:nt * P].rearrange("p (t f) -> p t f", t=nt))
            elif name == "mix":
                i = biased(xaT[:, lo_c:lo_c + n_c], o[:, 0:n_c], fcol[:, 3:4])
            elif name == "up":
                k, (lo_c, n_c) = part % KH, HALF[part // KH]
                if part == 0:
                    engine.wait_ge(expert_in, batch(it, off, 16, 16))
                i = biased(gT[:, k, lo_c:lo_c + n_c], o[:, 0:n_c], expert[:, 2 * HID + k:2 * HID + k + 1])
            elif name == "down":
                i = biased(yT[:, lo_c:lo_c + n_c], o[:, 0:n_c], expert[:, 2 * HID + KH:2 * HID + KH + 1])
            i.then_inc(spare_free[bank], 1)

        def iterations(engine, body):
            for j in range(-1, plan.loop[0]):
                body(Iteration(j))
            with engine.Fori(*plan.loop) as i:
                body(Iteration(i, plan.loop[0]))
            for j in range(plan.loop[1], B + 3):
                body(Iteration(j))

        block = ctx.enter_context(nc.Block())

        @block.sync
        def _(sp):
            sp.dma_start(mat[:], mats).then_inc(consts_in, 16)
            sp.dma_start(col[:], cols).then_inc(consts_in, 16)
            sp.dma_start(row[:], rows_in.unsqueeze(0).broadcast_to((P, NROW, D))).then_inc(consts_in, 16)
            sp.dma_start(xt[:], xT[0]).then_inc(x_in, 16)

            def done_alone(sp, it, offset, *units):
                for unit in units:
                    done(sp, it, offset, unit)
                    sp.sem_inc(passed, 1)

            def send_stacks(it, a, offset):
                alone(sp, split[a], batch(it, offset, 4, 4))
                for which, parts in ((0, (hi[a], hi[a], lo[a])), (1, (hi[a], lo[a], hi[a]))):
                    for s, part in enumerate(parts):
                        for h in range(H):
                            sp.dma_start(
                                stack[a][s * DK:(s + 1) * DK, which, h, :].bitcast(F32),
                                part[h * DK:(h + 1) * DK, which, :].bitcast(F32),
                            ).then_inc(stacked[a], 16)

            def body(it):
                if plan.has(it, -2):
                    if it.looped or it.like - 3 >= 0:
                        done_alone(sp, it, -3, ("down", 0), ("down", 1))
                    which = (it.index - 2) // 2
                    sp.dma_start(expert[:], experts[which]).then_inc(expert_in, 16)
                if plan.has(it, 2):
                    computed(sp, it, 1, "mdct", 1)
                    sp.sem_inc(passed, 1)
                    sp.dma_start(xt[:], xT[it.index + 2]).then_inc(x_in, 16)
                if plan.has(it, -1):
                    send_stacks(it, 1, -1)
                if plan.has(it, 1):
                    alone(sp, hx_ready, batch(it, 1, 2, 2))
                    sp.dma_start(spill[it.index + 1], hx[:].rearrange("p a c -> p (a c)")).then_inc(spill_out, 16)
                if plan.has(it, 1):
                    send_stacks(it, 0, 1)
                if plan.has(it, -3):
                    alone(sp, out_ready, batch(it, -3, 1, 1))
                    full = (NT - 1) * P
                    dst = out[it.index - 3]
                    sp.dma_start(dst[0:full].rearrange("(t p) f -> p t f", p=P), gz[:, 0:NT - 1, :]).then_inc(stored, 16)
                    sp.dma_start(dst[full:C], gz[0:C - full, NT - 1, :]).then_inc(stored, 16)
                if plan.has(it, -2):
                    if it.looped or it.like - 3 >= 0:
                        alone(sp, out_ready, batch(it, -3, 1, 1))
                    alone(sp, h2_ready, batch(it, -2, 1, 1))
                    sp.dma_start(h2_old[:], h2[:]).then_inc(h2_kept, 16)
                if plan.has(it, -1):
                    if it.looped or it.like - 2 >= 0:
                        alone(sp, h2_ready, batch(it, -2, 1, 1))
                    alone(sp, spill_out, batch(it, -1, 16, 16))
                    sp.dma_start(hxp[:].rearrange("p a c -> p (a c)"), spill[it.index - 1]).then_inc(spill_in, 16)

            iterations(sp, body)
            sp.wait_ge(stored, 32 * B)

        @block.tensor
        def _(pe):
            pe.wait_ge(consts_in, 48)
            for n, w in enumerate((wq2, wk2, wv2)):
                pe.matmul(spare[:, 0, n * P:(n + 1) * P], wo1, w, start=True, stop=True)
            pe.matmul(spare[:, 1, 0:1], wa, ln_b, start=True, stop=True)
            pe.matmul(spare[:, 1, 1:2], wo1_turned, bv1, start=True, stop=True).then_inc(prep_p, 1)
            pe.wait_ge(prep_v, 6)
            for n, w in enumerate((wq2, wk2, wv2)):
                mm = pe.matmul(spare[:, 1, 2 + n:3 + n], w, bo1, start=True, stop=True)
            mm.then_inc(prep_p, 1)
            pe.wait_ge(prep_v, 13)
            pe.matmul(spare[:, 1, P:2 * P], bv2_wide[:], wo2, start=True, stop=True).then_inc(prep_p, 1)
            pe.wait_ge(prep_v, 14)
            pe.wait_ge(prep_g, 4)

            def score(it, tile):
                phase, off, k, _ = tile
                t, h = divmod(k, H)
                n = plan.number(it, tile)
                if k == 0:
                    pe.wait_ge(stacked[phase], batch(it, off, 384, 384))
                if it.looped or n >= 2:
                    pe.wait_ge(probs_ready[k % 2], it.at(lambda j: (TILES * plan.phases_before(j - tile[3], phase) + k) // 2))
                m = rows(t)
                q = stack[phase][:, 0, h, t * P:t * P + m]
                kk = stack[phase][:, 1, h, :]
                pe.matmul(scores[0:m, k % 2, S0:S1], q, kk[:, 0:N0], start=True, stop=True)
                pe.matmul(scores[0:m, k % 2, S1:S0 + C], q, kk[:, N0:C], start=True, stop=True).then_inc(scores_full, 1)

            def turn(it, tile):
                phase, off, k, back = tile
                m = rows(k // H)
                n = plan.number(it, tile)
                pe.wait_ge(probs_ready[k % 2], it.at(lambda j: (TILES * plan.phases_before(j - back, phase) + k) // 2 + 1))
                for part, blocks in enumerate(((0, 1, 2), (3, 4))):
                    if it.looped or n >= 1:
                        pe.wait_ge(turned_free[part], n)
                    for b, j in enumerate(blocks):
                        mm = pe.transpose(turned[:, part, b * P:b * P + m], prob[0:m, k % PROBS, j * P:(j + 1) * P], ident[0:m, 0:m])
                    mm.then_inc(turned_full, 1)

            def values(it, phase, slot, n, u, blocks):
                name, _, part = u
                bank, _, _ = plan.bank(it, phase, slot, n)
                v, n_c = val[int(name[-1]) - 1], HALF[part][1]
                for j in blocks:
                    for h in range(H):
                        mm = pe.matmul(spare[h * DK:(h + 1) * DK, bank, 0:n_c], v[:, j, h * DK:(h + 1) * DK], probT[part][:, h, j, :],
                                       start=(j == 0), stop=(j == NT - 1))
                if NT - 1 in blocks:
                    mm.then_inc(spare_full[bank], 1)

            def unit(it, phase, slot, n, u):
                name, off, part = u
                bank, used, fresh = plan.bank(it, phase, slot, n)
                if it.looped or not fresh:
                    pe.wait_ge(spare_free[bank], used)
                o = spare[:, bank, :]
                lo_c, n_c = HALF[part] if part < 2 else (0, 0)
                a = 0 if name.endswith("1") else 1
                if name == "mdct":
                    if part == 0:
                        pe.wait_ge(x_in, batch(it, off, 16, 16))
                    for t in ((0, 1, 2, 3), (4,))[part]:
                        for c in (0, 1):
                            mm = pe.matmul(o[0:rows(t), (t % 4) * P:(t % 4 + 1) * P], xt[:, t * P + c:t * P + c + rows(t)],
                                           mdct[c], start=(c == 0), stop=(c == 1))
                elif name == "turn":
                    pe.wait_ge(x1_ready, batch(it, off, NT, NT))
                    for t in ((0, 1, 2, 3), (4,))[part]:
                        mm = pe.transpose(o[:, (t % 4) * P:(t % 4 + 1) * P], x1[:, t, :], ident[:])
                elif name == "turn_n":
                    pe.wait_ge(nrm_ready, batch(it, off, NT, NT))
                    for t in ((0, 1, 2, 3), (4,))[part]:
                        mm = pe.transpose(o[:, (t % 4) * P:(t % 4 + 1) * P], nrm[:, t, :], ident[:])
                elif name[0] in "qk":
                    if a == 0:
                        done(pe, it, off, ("turn", 0), ("turn", 1), bank=bank)
                        src, w = x1T, (wq1 if name[0] == "q" else wk1)
                    else:
                        done(pe, it, off, ("pv1", 0), ("pv1", 1), bank=bank)
                        src, w = attnT[0], wf[:, 0 if name[0] == "q" else 1, :]
                    mm = pe.matmul(o[:, 0:n_c], w, src[:, lo_c:lo_c + n_c], start=True, stop=True)
                elif name[0] == "v":
                    src, w = (x1T, wv1) if a == 0 else (attnT[0], wf[:, 2, :])
                    for t in ((0, 1, 2, 3), (4,))[part]:
                        mm = pe.matmul(o[0:rows(t), (t % 4) * P:(t % 4 + 1) * P], src[:, t * P:t * P + rows(t)], w, start=True, stop=True)
                elif name in ("spread1", "spread2"):
                    pe.wait_ge(wide_ready, attention_count(it, phase, part, 3, (1, 3)[part]))
                    for i, t in enumerate(HALF_TILES[part]):
                        m = rows(t)
                        mm = pe.matmul(o[:, i * P:i * P + m], rwide[0:m, i * H:(i + 1) * H, :].rearrange("p h d -> p (h d)"), ident[0:m, 0:m],
                                       start=True, stop=True)
                elif name in ("pv1", "pv2"):
                    last = (HALF_TILES[part][-1] + 1) * H
                    nn = attention_count(it, phase, part, TILES, last)
                    pe.wait_ge(turned_free[0], nn)
                    pe.wait_ge(turned_free[1], nn)
                    if part == 0:
                        done(pe, it, off, ("v" + name[-1], 0), ("v" + name[-1], 1), bank=bank)
                    values(it, phase, slot, n, u, plan.BLOCKS[0])
                    return
                elif name == "wo2":
                    done(pe, it, off, ("pv2", 0), ("pv2", 1), bank=bank)
                    for t in ((0, 1, 2, 3), (4,))[part]:
                        mm = pe.matmul(o[0:rows(t), (t % 4) * P:(t % 4 + 1) * P], attnT[1][:, t * P:t * P + rows(t)], wo2, start=True, stop=True)
                elif name == "mix":
                    done(pe, it, off, ("turn_n", 0), ("turn_n", 1), bank=bank)
                    pe.matmul(o[:, 0:n_c], wg[:], nrmT[:, lo_c:lo_c + n_c], start=True, stop=False)
                    for i, t in enumerate(HALF_TILES[part]):
                        m = rows(t)
                        mm = pe.matmul(o[:, i * P:i * P + m], xf[0:m, t, :], ident[0:m, 0:m], start=False, stop=(t == HALF_TILES[part][-1]))
                elif name == "up":
                    k, half = part % KH, part // KH
                    lo_c, n_c = HALF[half]
                    if k == 0:
                        done(pe, it, off, ("mix", half), bank=bank)
                    if part == 0:
                        pe.wait_ge(expert_in, batch(it, off, 16, 16))
                    mm = pe.matmul(o[:, 0:n_c], expert[:, k * P:(k + 1) * P], xaT[:, lo_c:lo_c + n_c], start=True, stop=True)
                elif name == "down":
                    pe.wait_ge(hidden_ready, batch(it, off, 1, 1))
                    for k in range(KH):
                        mm = pe.matmul(o[:, 0:n_c], expert[:, HID + k * D:HID + (k + 1) * D], gT[:, k, lo_c:lo_c + n_c],
                                       start=(k == 0), stop=(k == KH - 1))
                elif name == "next":
                    done(pe, it, off, ("down", 0), ("down", 1), bank=bank)
                    for t in ((0, 1, 2, 3), (4,))[part]:
                        mm = pe.matmul(o[0:rows(t), (t % 4) * P:(t % 4 + 1) * P], yT[:, t * P:t * P + rows(t)], wn, start=True, stop=True)
                mm.then_inc(spare_full[bank], 1)

            def body(it):
                for phase in (X, Y):
                    for slot in range(TILES):
                        for work in plan.ORDER["pe", phase]:
                            tile = plan.tile(it, phase, slot, LAG if work == "turn" else 0)
                            if work == "units":
                                now = slot - LEAD
                                for n, u in enumerate(plan.slot_units(it, phase, now)):
                                    unit(it, phase, now, n, u)
                                for step in range(1, len(plan.BLOCKS)):
                                    for n, u in enumerate(plan.slot_units(it, phase, now - step)):
                                        if u[0][:2] == "pv":
                                            values(it, phase, now - step, n, u, plan.BLOCKS[step])
                            elif tile:
                                (score if work == "score" else turn)(it, tile)

            iterations(pe, body)

        @block.scalar
        def _(act):
            def exponent(it, tile):
                phase, off, k, back = tile
                m = rows(k // H)
                n = plan.number(it, tile)
                if phase == 0:
                    act.wait_ge(top_found, batch(it, off, TILES, k + 1))
                    act.activation(nbias[0:m, k % 2:k % 2 + 1], top[0:m, k % 2, 0:1], ACT.Copy, scale=-1.0).then_inc(bias_ready[0], 1)
                act.wait_ge(bias_ready[phase], batch(it, off, TILES, k + 1))
                src = scores[0:m, k % 2, S0:S0 + C]
                bias = nbias[0:m, k % 2:k % 2 + 1]
                if phase == 0:
                    act.activation(expd[0:m, k % 2, :], src, ACT.Exp, bias=bias).then_inc(exp_done, 1)
                else:
                    if it.looped or n >= PROBS:
                        act.wait_ge(turned_full, 2 * n - 2 * PROBS + 2)
                    act.activation(prob[0:m, k % PROBS, 0:C], src, ACT.Exp, bias=bias,
                                   accum_out=rsum[0:m, k:k + 1]).then_inc(probs_ready[k % 2], 1)

            def unit(it, phase, slot, n, u):
                name, off, part = u
                if plan.taker(name, part) != "act":
                    return
                bank, used, _ = plan.bank(it, phase, slot, n)
                act.wait_ge(spare_full[bank], used + 1)
                take(act, act.copy, lambda o, i, b: act.activation(o, i, ACT.Identity, bias=b), it, name, off, part, bank)

            def copy_out(it, tile):
                for part in (0, 1):
                    if plan.COPIES[tile[0]][tile[2] % 4][part] == "act":
                        copy_block(act, act.copy, it, tile, part)

            def job(it, phase, slot, name, off, part):
                if name == "gelu_out":
                    act.wait_ge(z_biased, batch(it, off, 1, 1))
                    act.activation(gz[:], gz[:], ACT.Gelu).then_inc(gz_ready, 1)
                elif name == "gelu_up":
                    done(act, it, off, ("up", 2 * KH - 2), ("up", 2 * KH - 1))
                    act.activation(gT[:], gT[:], ACT.Gelu).then_inc(hidden_ready, 1)

            def body(it):
                for phase in (X, Y):
                    for slot in range(TILES):
                        tile = plan.tile(it, phase, slot)
                        if tile:
                            exponent(it, tile)
                        for work in plan.ORDER["act", phase]:
                            if work == "results":
                                for place, n, u in plan.results(it, phase, slot, "act"):
                                    unit(it, phase, place, n, u)
                            elif work == "copies":
                                tile = plan.tile(it, phase, slot, LAG)
                                if tile:
                                    copy_out(it, tile)
                            else:
                                for name, off, part in plan.JOBS[phase].get(slot, []):
                                    if plan.has(it, off):
                                        job(it, phase, slot, name, off, part)

            act.wait_ge(prep_v, 14)
            iterations(act, body)

        @block.vector
        def _(dve):
            for n, buf in enumerate((val[0], val[1], hraw, xf, z)):
                dve.memset(buf[:, NT - 1, :], 0.0).then_inc(prep_v, 1)
            dve.wait_ge(consts_in, 48)
            dve.wait_ge(prep_p, 1)
            dve.tensor_tensor(bo1, spare[:, 1, 1:2], bo1, ALU.add).then_inc(prep_v, 1)
            dve.tensor_scalar(wf[:, 0, :], spare[:, 0, 0:P], SCALE, None, ALU.mult).then_inc(prep_v, 1)
            dve.tensor_copy(wf[:, 1:3, :], spare[:, 0, P:3 * P].rearrange("p (n f) -> p n f", n=2)).then_inc(prep_v, 1)
            dve.tensor_scalar(wg[:], wa, ln_g, None, ALU.mult).then_inc(prep_v, 1)
            dve.tensor_scalar(wq1, wq1, SCALE, None, ALU.mult).then_inc(prep_v, 1)
            dve.tensor_scalar(fcol[:, 0:1], bq1, SCALE, None, ALU.mult).then_inc(prep_v, 1)
            dve.wait_ge(prep_p, 2)
            dve.tensor_tensor(fcol[:, 3:4], spare[:, 1, 0:1], battn, ALU.add)
            dve.tensor_scalar(fcol[:, 1:2], spare[:, 1, 2:3], bq2, SCALE, ALU.add, ALU.mult)
            dve.tensor_tensor(fcol[:, 2:3], spare[:, 1, 3:4], bk2, ALU.add)
            dve.tensor_tensor(bv2, spare[:, 1, 4:5], bv2, ALU.add).then_inc(prep_v, 1)
            dve.wait_ge(prep_v, 12)
            dve.tensor_copy(bv2_wide[:], bv2.broadcast_to((P, P))).then_inc(prep_v, 1)
            dve.wait_ge(prep_p, 3)
            dve.tensor_tensor(bo2_row, spare[:, 1, P:2 * P], bo2_row, ALU.add).then_inc(prep_v, 1)
            dve.wait_ge(prep_v, 14)

            def maximum(it, tile):
                phase, off, k, back = tile
                m = rows(k // H)
                n = plan.number(it, tile)
                src = scores[0:m, k % 2, S0:S0 + C]
                if phase == 0:
                    alone(dve, scores_full, n + 1)
                    dve.max(top[0:m, k % 2, :], src).then_inc(top_found, 1)
                else:
                    dve.wait_ge(scores_full, n + 1)
                    dve.tensor_reduce(nbias[0:m, k % 2:k % 2 + 1], src, AX.X, ALU.max, negate=True).then_inc(bias_ready[1], 1)

            def mask(it, tile):
                phase, off, k, back = tile
                if phase == 1:
                    return
                m = rows(k // H)
                n = plan.number(it, tile)
                if it.looped or n >= PROBS:
                    dve.wait_ge(turned_full, 2 * n - 2 * PROBS + 2)
                dve.wait_ge(exp_done, batch(it, off, TILES, k + 1))
                dve.scalar_tensor_tensor(prob[0:m, k % PROBS, 0:C], scores[0:m, k % 2, S0:S0 + C], top[0:m, k % 2, TOPK - 1:TOPK],
                                         expd[0:m, k % 2, :], ALU.is_ge, ALU.mult,
                                         accum_out=rsum[0:m, k:k + 1]).then_inc(probs_ready[k % 2], 1)

            def copy_out(it, tile):
                for part in (0, 1):
                    if plan.COPIES[tile[0]][tile[2] % 4][part] == "dve":
                        copy_block(dve, dve.tensor_copy, it, tile, part)

            def job(it, phase, slot, name, off, part):
                if name in ("inverse1", "inverse2"):
                    a = 0 if name == "inverse1" else 1
                    tiles = HALF_TILES[part]
                    k0, k1 = tiles[0] * H, (tiles[-1] + 1) * H
                    for par in (0, 1):
                        dve.wait_ge(probs_ready[par], attention_count(it, phase, part, TILES // 2, k1 // 2))
                    groups = ((0, 3),) if part == 0 else ((3, 4), (4, 5))
                    for t0, t1 in groups:
                        m = rows(t0)
                        dve.reciprocal(rinv[0:m, t0 * H:t1 * H], rsum[0:m, t0 * H:t1 * H]).then_inc(inverse_found, 1)
                    before = half_before(it, off, a, part)
                    if before:
                        computed(dve, it, before[1], before[0][0].replace("pv", "spread"), before[0][1])
                    dve.wait_ge(inverse_found, attention_count(it, phase, part, 3, (1, 3)[part]))
                    for t0, t1 in groups:
                        m, at = rows(t0), (t0 - tiles[0]) * H
                        dve.tensor_copy(rwide[0:m, at:at + (t1 - t0) * H, :],
                                        rinv[0:m, t0 * H:t1 * H].unsqueeze(2).broadcast_to((m, (t1 - t0) * H, DK))).then_inc(wide_ready, 1)
                elif name in ("stats_h", "stats_hh", "stats_h2"):
                    s, buf = {"stats_h": (0, hraw), "stats_hh": (1, hh), "stats_h2": (2, h2)}[name]
                    if s == 0:
                        done(dve, it, off, ("mdct", 0), ("mdct", 1))
                    elif s == 1:
                        dve.wait_ge(hh_ready, batch(it, off, 1, 1))
                    else:
                        dve.wait_ge(h2_ready, batch(it, off, 1, 1))
                    for t in range(NT):
                        dve.bn_stats(stat[:, s, t, :], buf[:, t, :]).then_inc(stats_part[s], 1)

            def unit(it, phase, slot, n, u):
                name, off, part = u
                if plan.taker(name, part) != "dve":
                    return
                bank, used, _ = plan.bank(it, phase, slot, n)
                dve.wait_ge(spare_full[bank], used + 1)
                if name in plan.TAKER:
                    take(dve, dve.tensor_copy, lambda o, i, b: dve.tensor_scalar(o, i, b, None, ALU.add), it, name, off, part, bank)
                else:
                    lo_c, n_c = HALF[part]
                    done(dve, it, off, ("spread" + name[-1], part))
                    dve.tensor_tensor(attnT[int(name[-1]) - 1][:, lo_c:lo_c + n_c], spare[:, bank, 0:n_c], spread[:, 0:n_c],
                                      ALU.mult).then_inc(spare_free[bank], 1)

            def body(it):
                for phase in (X, Y):
                    for slot in range(TILES):
                        tile = plan.tile(it, phase, slot)
                        if tile:
                            maximum(it, tile)
                        tile = plan.tile(it, phase, slot, 1)
                        if tile and slot % 2:
                            mask(it, tile)
                        for work in plan.ORDER["dve", phase]:
                            if work == "results":
                                for place, n, u in plan.results(it, phase, slot, "dve"):
                                    unit(it, phase, place, n, u)
                            elif work == "mask":
                                tile = plan.tile(it, phase, slot)
                                if tile and slot % 2:
                                    mask(it, tile)
                            elif work == "copies":
                                tile = plan.tile(it, phase, slot, LAG)
                                if tile:
                                    copy_out(it, tile)
                            else:
                                for name, off, part in plan.JOBS[phase].get(slot, []):
                                    if plan.has(it, off):
                                        job(it, phase, slot, name, off, part)

            iterations(dve, body)

        @block.gpsimd
        def _(pool):
            pool.memset(ident[:], 0.0).then_inc(prep_g, 1)
            pool.memset(half_neg[:], -0.5).then_inc(prep_g, 1)
            pool.memset(prob[:, :, C:CP], 0.0).then_inc(prep_g, 1)
            pool.wait_ge(prep_g, 3)
            pool.affine_select(out=ident[:], in_=ident[:], compare_op=ALU.not_equal, fill=1.0, base=0,
                               pattern=[[-1, P]], channel_multiplier=1).then_inc(prep_g, 1)

            def norm(it, off, s, step, k):
                def before(n):
                    alone(pool, step, batch(it, off, STEPS[s], k + n))
                means, squares = (stat[:, s, :, 1], stat[:, s, :, 4]), (stat[:, s, :, 2], stat[:, s, :, 5])
                total, diff, both, apart, within = (part[:, s, n, :] for n in range(5))
                alone(pool, stats_part[s], batch(it, off, NT, NT))
                pool.tensor_tensor(total, means[0], means[1], ALU.add).then_inc(step, 1)
                pool.tensor_tensor(diff, means[0], means[1], ALU.subtract).then_inc(step, 1)
                pool.tensor_tensor(both, squares[0], squares[1], ALU.add).then_inc(step, 1)
                before(2)
                pool.tensor_tensor(apart, diff, diff, ALU.mult).then_inc(step, 1)
                before(3)
                pool.tensor_scalar(within, both, 1.0 / D, 0.0, ALU.mult, ALU.add).then_inc(step, 1)
                before(4)
                pool.tensor_scalar(diff, apart, 0.25, 0.0, ALU.mult, ALU.add).then_inc(step, 1)
                before(6)
                pool.tensor_tensor(var[:, s, :], diff, within, ALU.add).then_inc(step, 1)
                before(7)
                pool.tensor_scalar(ve[:, s, :], var[:, s, :], EPS, 1.0, ALU.add, ALU.mult).then_inc(step, 1)
                before(8)
                pool.tensor_tensor(rstd[:, s, :], ve[:, s, :], half_neg[:], ALU.pow).then_inc(step, 1)
                before(9)
                pool.tensor_tensor(negm[:, s, :], total, rstd[:, s, :], ALU.mult).then_inc(step, 1)
                before(10)
                pool.tensor_scalar(shift[:, s, :], negm[:, s, :], -0.5, 1.0, ALU.mult, ALU.mult).then_inc(step, 1)
                before(NORM)

            def scaled(dst, src, scale, add, ready):
                for t in range(NT):
                    pool.tensor_scalar(dst[:, t, :], src[:, t, :], scale[:, t:t + 1],
                                       add if isinstance(add, float) else add[:, t:t + 1], ALU.mult, ALU.add).then_inc(ready, 1)

            def wide(r):
                return r.unsqueeze(1).broadcast_to((P, NT, D))

            hx_t = hx[:].rearrange("p a (t f) -> p a t f", t=NT)
            hxp_t = hxp[:].rearrange("p a (t f) -> p a t f", t=NT)

            def front(it, off):
                norm(it, off, 0, norm_step[0], 0)
                if it.looped or it.like + off >= 1:
                    computed(pool, it, off - 1, "turn", 1)
                    pool.sem_inc(passed, 1)
                scaled(x1, hraw, rstd[:, 0, :], shift[:, 0, :], x1_ready)
                if it.looped or it.like + off >= 1:
                    alone(pool, spill_out, batch(it, off, 16, 0))
                pool.tensor_tensor(hx_t[:, 0], hraw[:], wide(beta_row), ALU.add).then_inc(hx_ready, 1)
                pool.wait_ge(x1_ready, batch(it, off, NT, NT))
                pool.tensor_tensor(hx_t[:, 1], x1[:], wide(bo2_row), ALU.add).then_inc(hx_ready, 1)

            def post(it, off):
                done(pool, it, off, ("wo2", 0), ("wo2", 1))
                pool.wait_ge(spill_in, batch(it, off, 16, 16))
                pool.tensor_tensor(hh[:], xf[:], hxp_t[:, 1], ALU.add).then_inc(hh_ready, 1)
                norm(it, off, 1, norm_step[1], 0)
                scaled(xf, hh, rstd[:, 1, :], shift[:, 1, :], norm_step[1])
                pool.wait_ge(norm_step[1], batch(it, off, STEPS[1], NORM + NT))
                pool.tensor_tensor(xf[:], xf[:], wide(gamma_row), ALU.mult).then_inc(norm_step[1], 1)
                if it.looped or it.like + off >= 1:
                    pool.wait_ge(h2_kept, batch(it, off, 16, 0))
                pool.wait_ge(norm_step[1], batch(it, off, STEPS[1], NORM + 1 + NT))
                pool.tensor_tensor(h2[:], xf[:], hxp_t[:, 0], ALU.add).then_inc(h2_ready, 1)

                step = norm_step[2]
                norm(it, off, 2, step, 0)
                pool.tensor_tensor(var_x[:, 0, :], var[:, 2, :], rstd[:, 2, :], ALU.mult).then_inc(step, 1)
                pool.wait_ge(step, batch(it, off, STEPS[2], NORM + 1))
                pool.tensor_tensor(var_x[:, 1, :], var_x[:, 0, :], rstd[:, 2, :], ALU.mult).then_inc(step, 1)
                alone(pool, step, batch(it, off, STEPS[2], NORM + 2))
                pool.tensor_scalar(var_x[:, 0, :], var_x[:, 1, :], EPS, 1.0, ALU.add, ALU.mult).then_inc(step, 1)
                pool.wait_ge(step, batch(it, off, STEPS[2], NORM + 3))
                pool.tensor_tensor(rstd_x[:], var_x[:, 0, :], half_neg[:], ALU.pow).then_inc(step, 1)
                scaled(xf, h2, rstd[:, 2, :], shift[:, 2, :], step)
                if it.looped or it.like + off >= 1:
                    computed(pool, it, off - 1, "turn_n", 1)
                    pool.sem_inc(passed, 1)
                alone(pool, step, batch(it, off, STEPS[2], NORM + 4 + NT))
                scaled(nrm, xf, rstd_x, 0.0, nrm_ready)

            def split_operands(it, off, a):
                for w in (0, 1):
                    for part in (0, 1):
                        done(pool, it, off, ("qk"[w] + "12"[a], part))
                        pool.sem_inc(passed, 1)
                    pool.tensor_scalar(hi[a][:, w, :], lo[a][:, w, :].bitcast(F32), 1.0, 0.0, ALU.mult, ALU.add).then_inc(split[a], 1)
                for w in (0, 1):
                    pool.wait_ge(split[a], batch(it, off, 4, 1 + w))
                    whole = lo[a][:, w, :].bitcast(F32)
                    pool.tensor_tensor(lo[a][:, w, :], whole, hi[a][:, w, :].bitcast(F32), ALU.subtract).then_inc(split[a], 1)

            def final(it, off):
                done(pool, it, off, ("next", 0), ("next", 1))
                if it.looped or it.like + off >= 1:
                    pool.wait_ge(stored, batch(it, off, 32, 0))
                pool.tensor_tensor(gz[:], z[:], wide(next_row), ALU.add).then_inc(z_biased, 1)
                pool.wait_ge(gz_ready, batch(it, off, 1, 1))
                pool.wait_ge(h2_kept, batch(it, off, 16, 16))
                pool.tensor_tensor(gz[:], gz[:], h2_old[:], ALU.add).then_inc(out_ready, 1)

            def body(it):
                if plan.has(it, 1):
                    front(it, 1)
                if plan.has(it, -1):
                    split_operands(it, -1, 1)
                if plan.has(it, -2):
                    post(it, -2)
                if plan.has(it, 1):
                    split_operands(it, 1, 0)
                if plan.has(it, -3):
                    final(it, -3)

            pool.wait_ge(consts_in, 48)
            pool.wait_ge(prep_v, 14)
            iterations(pool, body)


def kernel(**inputs):
    import concourse.bacc as bacc
    from concourse.bass_utils import run_bass_kernel_spmd

    arr = {k: np.ascontiguousarray(v) for k, v in inputs.items()}
    attn = {k[len("L0_attn_"):]: v for k, v in arr.items() if k.startswith("L0_attn_")}
    ffn = {k[len("L0_ffn_"):]: v for k, v in arr.items() if k.startswith("L0_ffn_")}
    x = arr["x"]
    batches, samples = x.shape

    blocks = np.zeros((batches, C + 1, P), np.float32)
    blocks.reshape(batches, -1)[:, P:P + samples] = x
    xT = np.ascontiguousarray(blocks.transpose(0, 2, 1))

    length = 2 * P
    n = np.arange(length, dtype=np.float32) + np.float32(0.5)
    k = np.float32(np.pi / P) * n[:P]
    table = np.sqrt(np.float32(4.0 / P)) * np.cos((n + np.float32(P / 2))[:, None] * k[None, :])
    window = np.sin(np.float32(np.pi) * n / np.float32(length))
    mdct = (window[:, None] * table).astype(np.float32)

    mats = np.ascontiguousarray(np.stack(
        [attn["Wq1"].T, attn["Wk1"].T, attn["Wv1"].T, attn["Wo1"], attn["Wq2"].T, attn["Wk2"].T, attn["Wv2"].T,
         attn["Wo2"].T, ffn["attn_w"].T, ffn["next_w"].T, mdct[:P], mdct[P:], attn["Wo1"].T], axis=1))
    cols = np.ascontiguousarray(np.stack(
        [attn["bq1"], attn["bk1"], attn["bo1"], attn["bq2"], attn["bk2"], ffn["ln_g"], ffn["ln_b"], ffn["attn_b"],
         attn["bv1"], attn["bv2"]], axis=1))
    rows_in = np.stack([attn["bo2"], attn["gamma"], attn["beta"], ffn["next_b"]])
    e = ffn["fc1_w"].shape[0]
    experts = np.concatenate(
        [ffn["fc1_w"].transpose(0, 2, 1),
         ffn["fc2_w"].transpose(0, 2, 1).reshape(e, KH, P, D).transpose(0, 2, 1, 3).reshape(e, P, KH * D),
         ffn["fc1_b"].reshape(e, KH, P).transpose(0, 2, 1), ffn["fc2_b"][:, :, None]], axis=2)
    experts = np.ascontiguousarray(np.concatenate([experts, experts]))

    given = {"xT": xT, "mats": mats, "cols": cols, "rows_in": rows_in, "experts": experts}
    nc = bacc.Bacc("TRN2", target_bir_lowering=False, num_devices=1)
    aps = {name: nc.dram_tensor(name, a.shape, F32, kind="ExternalInput").ap() for name, a in given.items()}
    out = nc.dram_tensor("out", (batches, C, D), F32, kind="ExternalOutput").ap()
    build(nc, **aps, out=out)
    result = run_bass_kernel_spmd(nc, [given], core_ids=[0])
    return result.results[0]["out"]
```
